# Optimizing a Trainium2 kernel written in Bass

```python
import numpy as np
import jax
import jax.numpy as jnp

def _softmax(x, axis=-1):
    return jax.nn.softmax(x, axis=axis)

def _gelu(x):
    return jax.nn.gelu(x, approximate=True)

def _silu(x):
    return jax.nn.silu(x)

def _sigmoid(x):
    return jax.nn.sigmoid(x)

def _layernorm(x, axis=-1, eps=1e-05):
    m = jnp.mean(x, axis=axis, keepdims=True)
    v = jnp.var(x, axis=axis, keepdims=True)
    return (x - m) / jnp.sqrt(v + eps)

def _scatter_add(tgt, idx, src, axis=0):
    return tgt.at[idx].add(src)

def _segment_sum(src, seg, n):
    return jax.ops.segment_sum(src, seg, n)
kernel_name = 'mk_gnn_resnorm_d2_gnn_r16_efde8f'

def setup_inputs(seed: int=0):
    np.random.seed(seed)
    _w = jnp.asarray

    def _rec_inputs():
        import jax
        import jax.numpy as jnp
        _gk = jax.random.key(seed)
        x = -6.415e-05 + 1 * jax.random.normal(jax.random.fold_in(_gk, 1), (625, 1024), jnp.float32)
        src = jax.random.randint(jax.random.fold_in(_gk, 2), (20000,), 0, 625, jnp.int32)
        dst = jax.random.randint(jax.random.fold_in(_gk, 3), (20000,), 0, 625, jnp.int32)
        _o = jnp.argsort(dst, stable=True)
        src = src[_o]
        dst = dst[_o]
        edge_type_8 = jax.random.randint(jax.random.fold_in(_gk, 13), (20000,), 0, 8, jnp.int32)
        return (x, src, dst, edge_type_8)
    x, src, dst, edge_type_8 = _rec_inputs()

    def _L0_gnn_setup():
        import jax, jax.numpy as jnp
        import numpy as np
        NEG_SLOPE = 0.1
        EPS = 1e-05
        key = jax.random.key(seed)
        k1, k2, k3, k4, k5 = jax.random.split(key, 5)
        N, E, DIN, DOUT = (625, 10000, 1024, 1024)
        x = jax.random.normal(k1, (N, DIN), dtype=jnp.float32)
        W = jax.random.normal(k2, (DIN, DOUT), dtype=jnp.float32) * 0.02
        a = jax.random.normal(k3, (1, 2 * DOUT), dtype=jnp.float32) * 0.02
        src = jax.random.randint(k4, (E,), 0, N, dtype=jnp.int64)
        dst = jax.random.randint(k5, (E,), 0, N, dtype=jnp.int64)
        return {'x': x, 'W': W, 'a': a, 'src': src, 'dst': dst}
    _L0_gnn_all = _L0_gnn_setup()
    _L0_gnn_in = {k: v for k, v in _L0_gnn_all.items() if k in ('W', 'a')}
    del _L0_gnn_all

    def _L1_gnn_setup():
        import jax, jax.numpy as jnp
        import numpy as np
        N, D, R, E = (625, 1024, 8, 5000)

        def _rgcn(x, edge_index, edge_type, weight, root, bias):
            src, dst = (edge_index[0], edge_index[1])
            msgs = x[src]
            out = x @ root + bias
            n = x.shape[0]
            for r in range(weight.shape[0]):
                mask = (edge_type == r).astype(x.dtype)
                sums = jax.ops.segment_sum(msgs * mask[:, None], dst, num_segments=n)
                cnt = jax.ops.segment_sum(mask, dst, num_segments=n)
                mean = sums / jnp.maximum(cnt, 1.0)[:, None]
                out = out + mean @ weight[r]
            return out
        key = jax.random.key(seed)
        ks = jax.random.split(key, 8)
        s = 1.0 / np.sqrt(D)
        x = jax.random.normal(ks[0], (N, D), dtype=jnp.float32)
        edge_index = jax.random.randint(ks[1], (2, E), 0, N, dtype=jnp.int64)
        edge_type = jax.random.randint(ks[2], (E,), 0, R, dtype=jnp.int64)
        weight = jax.random.normal(ks[3], (R, D, D), dtype=jnp.float32) * s
        root = jax.random.normal(ks[4], (D, D), dtype=jnp.float32) * s
        bias = jnp.zeros((D,), dtype=jnp.float32)
        w_gate = jax.random.normal(ks[5], (2 * D, D), dtype=jnp.float32) * (1.0 / np.sqrt(2 * D))
        b_gate = jnp.zeros((D,), dtype=jnp.float32)
        return {'x': x, 'edge_index': edge_index, 'edge_type': edge_type, 'weight': weight, 'root': root, 'bias': bias, 'w_gate': w_gate, 'b_gate': b_gate}
    _L1_gnn_all = _L1_gnn_setup()
    _L1_gnn_in = {k: v for k, v in _L1_gnn_all.items() if k in ('weight', 'root', 'bias', 'w_gate', 'b_gate')}
    del _L1_gnn_all
    return {'x': x, 'src': src, 'dst': dst, 'edge_type_8': edge_type_8, 'L0_gnn_W': _L0_gnn_in['W'], 'L0_gnn_a': _L0_gnn_in['a'], 'L1_gnn_weight': _L1_gnn_in['weight'], 'L1_gnn_root': _L1_gnn_in['root'], 'L1_gnn_bias': _L1_gnn_in['bias'], 'L1_gnn_w_gate': _L1_gnn_in['w_gate'], 'L1_gnn_b_gate': _L1_gnn_in['b_gate']}

def reference(x, src, dst, edge_type_8, L0_gnn_W, L0_gnn_a, L1_gnn_weight, L1_gnn_root, L1_gnn_bias, L1_gnn_w_gate, L1_gnn_b_gate):
    import jax
    import jax.numpy as jnp

    def _L0_gnn_ref(x, W, a, src, dst):
        import jax, jax.numpy as jnp
        import numpy as np
        NEG_SLOPE = 0.1
        EPS = 1e-05
        N = x.shape[0]
        d = W.shape[1]
        h = x @ W
        a_l, a_r = (a[0, :d], a[0, d:])
        al = h @ a_l
        ar = h @ a_r
        e = jnp.exp(-jax.nn.leaky_relu(al[src] + ar[dst], negative_slope=NEG_SLOPE))
        rowsum = jax.ops.segment_sum(e, src, num_segments=N)
        h_prime = jax.ops.segment_sum(e[:, None] * h[dst], src, num_segments=N)
        h_prime = h_prime / (rowsum[:, None] + EPS)
        return jax.nn.elu(h_prime)

    def _L1_gnn_ref(x, edge_index, edge_type, weight, root, bias, w_gate, b_gate):
        import jax, jax.numpy as jnp
        import numpy as np
        N, D, R, E = (625, 1024, 8, 5000)

        def _rgcn(x, edge_index, edge_type, weight, root, bias):
            src, dst = (edge_index[0], edge_index[1])
            msgs = x[src]
            out = x @ root + bias
            n = x.shape[0]
            for r in range(weight.shape[0]):
                mask = (edge_type == r).astype(x.dtype)
                sums = jax.ops.segment_sum(msgs * mask[:, None], dst, num_segments=n)
                cnt = jax.ops.segment_sum(mask, dst, num_segments=n)
                mean = sums / jnp.maximum(cnt, 1.0)[:, None]
                out = out + mean @ weight[r]
            return out
        u = _rgcn(x, edge_index, edge_type, weight, root, bias)
        z = jnp.concatenate([u, x], axis=1) @ w_gate + b_gate
        h = jnp.tanh(u) * z + x * (1.0 - z)
        return h
    edge_index = jnp.stack([src, dst])
    x = _layernorm(x + _L0_gnn_ref(x, L0_gnn_W, L0_gnn_a, src, dst), axis=-1)
    x = _layernorm(x + _L1_gnn_ref(x, edge_index, edge_type_8, L1_gnn_weight, L1_gnn_root, L1_gnn_bias, L1_gnn_w_gate, L1_gnn_b_gate), axis=-1)
    return x

_drawn_inputs = setup_inputs


def setup_inputs(seed=0):
    import zlib

    import numpy as np

    out = dict(_drawn_inputs(seed))
    spreads = {'L1_gnn_bias': (0.0, 0.1), 'L1_gnn_b_gate': (0.0, 0.1)}
    factors = {}
    for name, (base, spread) in spreads.items():
        noise = np.random.default_rng([zlib.crc32(name.encode()), seed]).standard_normal(out[name].shape)
        drawn = base * np.exp(spread * noise) if base else spread * noise
        out[name] = jnp.asarray(drawn.astype(out[name].dtype))
    for name, factor in factors.items():
        out[name] = (out[name] * factor).astype(out[name].dtype)
    return out
```

```python
import concourse.bass as bass
from concourse import mybir
from contextlib import ExitStack


def gat_rgcn_kernel(nc, dst_cols, src_cols, type_cols, dst_units, xT, x, weights, a, bias, b_gate, counts_dram, out):
    f32 = mybir.dt.float32
    f32r = mybir.dt.float32r
    bf16 = mybir.dt.bfloat16
    f16 = mybir.dt.float16
    i32 = mybir.dt.int32
    i16 = mybir.dt.int16
    ALU = mybir.AluOpType
    ACT = mybir.ActivationFunctionType
    X = mybir.AxisListType.X
    ds = bass.ds

    N, D = x.shape
    P = 128
    KT = D // P
    NT = -(-N // P)
    NP = NT * P
    H2 = D // 2
    R = counts_dram.shape[0]
    EPS = 1e-5
    SLOPE = 0.1
    FLT_MAX = 3.4028234e38

    TILES = dst_cols.shape[1]
    PAIR = 2
    UNITS = dst_units.shape[0]
    WIN = P // R
    WINDOWS = NP // WIN
    GROUP = P // WIN
    SPLIT = 320
    NE = N + N % 2
    NCOL = [(0, SPLIT), (SPLIT, NE - SPLIT)]

    RING = 4
    STEPS = R + 1
    ITEMS = 2 + 2 * KT
    GB = 3
    MEANS = 2 * KT

    def rows(t):
        return P if t < NT - 1 else N - P * (NT - 1)

    ctx = ExitStack()
    with ctx:
        def sem(name):
            return ctx.enter_context(nc.semaphore(name))

        def sb(name, shape, dt, where=ctx):
            return where.enter_context(nc.sbuf_tensor(name, shape, dt))

        M_hi = [sb("M_hi0", [P, KT, NP], f32r), None]
        M_lo = [sb(f"M_lo{b}", [P, KT, NP], f32r) for b in range(2)]
        w_raw = [sb(f"w_raw{b}", [P, H2], f32) for b in range(RING)]
        w_hi = [sb(f"w_hi{b}", [P, H2], f32r) for b in range(RING)]
        w_lo = [sb(f"w_lo{b}", [P, H2], f32r) for b in range(RING)]
        ident = sb("ident", [P, P], f32)
        ones = sb("ones", [P, P], f32)
        ones_r = sb("ones_r", [P, P], f32r)
        eps_col = sb("eps_col", [P, 1], f32)
        alr = sb("alr", [P, 2 * NT], f32)
        rowsum = sb("rowsum", [P, NT], f32)
        mv = sb("mv", [P, NT, 2], f32)
        rstd = sb("rstd", [P, NT], f32)
        stats = sb("stats", [P, 2, 2, 6], f32)

        with ExitStack() as counting:
            ints = sb("ints", [P, 3, TILES], i32, counting)
            src_f = sb("src_f", [P, TILES], f32, counting)
            q_f = sb("q_f", [P, TILES], f32, counting)
            type_f = sb("type_f", [P, TILES], f32, counting)
            units_i = sb("units_i", [UNITS, PAIR * P], i32, counting)
            unit_mm = sb("unit_mm", [UNITS, 2], f32, counting)
            unit_diag = sb("unit_diag", [UNITS, 2, UNITS + 1], f32, counting)
            iota_up = sb("iota_up", [P, UNITS], f32, counting)
            iota_down = sb("iota_down", [P, UNITS], f32, counting)
            reach = sb("reach", [WINDOWS, 2, UNITS], f32, counting)
            lohi = sb("lohi", [WINDOWS, 4], f32, counting)
            lohi_row = sb("lohi_row", [1, 2 * WINDOWS], i32, counting)
            win_edge = sb("win_edge", [P, 2], f32, counting)
            part_col = sb("part_col", [P, 1], f32, counting)
            win_base = sb("win_base", [P, WINDOWS], f32, counting)
            iota_node = sb("iota_node", [P, NP], f16, counting)
            zeros = sb("zeros", [P, P], bf16, counting)
            hot_src = [sb(f"hot_src{s}", [P, NP], bf16, counting) for s in range(PAIR)]
            hot_q = [sb(f"hot_q{s}", [P, P], bf16, counting) for s in range(PAIR)]
            win_sb = [sb(f"win_sb{b}", [P, NP], f32, counting) for b in range(2)]
        M_hi[1] = sb("M_hi1", [P, KT, NP], f32r)
        h_hi = M_hi[1][:, :, :].rearrange("p a b -> p (a b)").rearrange("p (t n) -> p t n", t=NT)
        h_lo = M_lo[1][:, :, :].rearrange("p a b -> p (a b)").rearrange("p (t n) -> p t n", t=NT)

        with ExitStack() as early:
            counts = sb("counts", [P, NT, R, NP], i16, early)
            counts_all = sb("counts_all", [P, NT, NP], i16, early)
            iota_i = sb("iota_i", [P, NP], i32, early)
            junk = sb("junk", [P, H2], f32, early)
            dots = sb("dots", [P, 2, 2 * NT], f32, early)
            diag = sb("diag", [P, NT, P], f32, early)
            with ExitStack() as first:
                xT_raw = sb("xT_raw", [P, KT, N], f32, first)
            with ExitStack() as first:
                sums = sb("sums", [P, NT, R // 2, NP], i16, first)
            att = sb("att", [P, NT, NP], f32, early)
            a_bc = sb("a_bc", [P, 2 * D], f32, early)

        with ExitStack() as late:
            x1_hi = sb("x1_hi", [P, NT, D], f32r, late)
            x1_lo = sb("x1_lo", [P, NT, D], f32r, late)
            u = sb("u", [P, NT, D], f32, late)
            bias_bc = sb("bias_bc", [P, D], f32, late)
            bg_bc = sb("bg_bc", [P, D], f32, late)
            with ExitStack() as elu:
                gt = [sb(f"gt{b}", [P, D], f32, elu) for b in range(2)]
                et = [sb(f"et{b}", [P, D], f32, elu) for b in range(2)]
            with ExitStack() as agg:
                C_hi = sb("C_hi", [P, NT, NP], f32r, agg)
                inv = sb("inv", [P, NE], f32, agg)
                mt = [sb(f"mt{b}", [P, SPLIT], f32, agg) for b in range(4)]
                c16 = sb("c16", [P, NT, NP], i16, agg)
            with ExitStack() as final:
                xf = sb("xf", [P, NT, D], f32, final)
                zt = [sb(f"zt{b}", [P, H2], f32, final) for b in range(2)]

        ps = ctx.enter_context(nc.psum_tensor("ps", [P, 8 * H2], f32))

        def bank(b, p=P, c0=0, c=H2):
            return ps[0:p, b * H2 + c0:b * H2 + c0 + c]

        def pair(b, p=P):
            return ps[0:p, 2 * b * H2:2 * (b + 1) * H2]

        edges_here = sem("edges_here")
        xT_here = sem("xT_here")
        a_here = sem("a_here")
        bias_here = sem("bias_here")
        x_here = sem("x_here")
        raw_here = [sem(f"raw_here{b}") for b in range(RING)]
        w_hi_done = sem("w_hi_done")
        w_lo_done = sem("w_lo_done")
        w_used = sem("w_used")
        pool_consts = sem("pool_consts")
        pool_step = sem("pool_step")
        dve_step = sem("dve_step")
        act_step = sem("act_step")
        consts_done = sem("consts_done")
        units_diag_done = sem("units_diag_done")
        units_bcast = sem("units_bcast")
        lohi_done = sem("lohi_done")
        lohi_turned = sem("lohi_turned")
        row_done = sem("row_done")
        built = [sem(f"built{s}") for s in range(PAIR)]
        slot_free = [sem(f"slot_free{s}") for s in range(PAIR)]
        window_counted = sem("window_counted")
        window_copied = sem("window_copied")
        turned = sem("turned")
        turned_read = sem("turned_read")
        flushed = sem("flushed")
        summed = sem("summed")
        xT_hi_done = sem("xT_hi_done")
        xT_lo_done = sem("xT_lo_done")
        u_ready = sem("u_ready")
        u_drained = sem("u_drained")
        h_hi_done = sem("h_hi_done")
        diag_done = sem("diag_done")
        ar_bcast = sem("ar_bcast")
        sum_done = sem("sum_done")
        leaky_done = sem("leaky_done")
        exp_done = sem("exp_done")
        att_done = sem("att_done")
        attT_ready = sem("attT_ready")
        attT_hi_done = sem("attT_hi_done")
        attT_lo_done = sem("attT_lo_done")
        hp_ready = sem("hp_ready")
        elu_in = sem("elu_in")
        hp_read = sem("hp_read")
        elu_exp = sem("elu_exp")
        y_done = sem("y_done")
        std_done = sem("std_done")
        x1_done = sem("x1_done")
        x1_hi_done = sem("x1_hi_done")
        x1_lo_done = sem("x1_lo_done")
        x1T_ready = sem("x1T_ready")
        x1T_hi_done = sem("x1T_hi_done")
        x1T_lo_done = sem("x1T_lo_done")
        u_init = sem("u_init")
        c16_here = sem("c16_here")
        C_ready = sem("C_ready")
        g_ready = sem("g_ready")
        g_drained = sem("g_drained")
        inv_ready = sem("inv_ready")
        m_hi_done = sem("m_hi_done")
        m_lo_done = sem("m_lo_done")
        xt2_ready = sem("xt2_ready")
        xt2_hi_done = sem("xt2_hi_done")
        xt2_lo_done = sem("xt2_lo_done")
        uT_ready = sem("uT_ready")
        uT_hi_done = sem("uT_hi_done")
        uT_lo_done = sem("uT_lo_done")
        tanh_done = sem("tanh_done")
        xf_done = sem("xf_done")
        d_done = sem("d_done")
        var_done = sem("var_done")
        std2_done = sem("std2_done")
        y2_done = sem("y2_done")
        out_done = sem("out_done")

        SEG_W = 0
        SEG_U = 2
        SEG_G = SEG_U + 2 * STEPS
        SEGS = SEG_G + 4
        BANKS_G = NT * (SEG_G)

        def chunk_rows(n, k):
            if n < SEG_G:
                return (n // 2) * D + k * P, (n % 2) * H2
            m = n - SEG_G
            return (STEPS + 1 + (1 - m % 2)) * D + k * P, (m // 2) * H2

        def closes(n):
            return not isinstance(n, int) or n < SEG_G or n % 2 == 1

        def used_before(n):
            if not isinstance(n, int) or n < SEG_G:
                return n * (KT - 1)
            return SEG_G * (KT - 1) + (n - SEG_G) * KT - (n - SEG_G) // 2

        def filled(n):
            if not isinstance(n, int) or n < SEG_G:
                return n * NT + NT
            return BANKS_G + NT * ((n - SEG_G) // 2 + 1)

        block = ctx.enter_context(nc.Block())

        @block.sync
        def _(sp):
            def load_chunk(n, k, at=None, first=False):
                if not first:
                    sp.wait_ge(w_lo_done, 8 * n + k - RING + 1)
                r0, c0 = at or chunk_rows(n, k)
                sp.dma_start(w_raw[k % RING][:, :], weights[ds(r0, P), c0:c0 + H2]).then_inc(raw_here[k % RING], 16)

            def load_ahead(n, last=False):
                for k in range(KT):
                    if k < KT - RING:
                        load_chunk(n, k + RING)
                    elif not last:
                        load_chunk(n + 1, k + RING - KT)

            sp.dma_start(ints[:, 0, :], dst_cols).then_inc(edges_here, 16)
            sp.dma_start(ints[:, 1, :], src_cols).then_inc(edges_here, 16)
            sp.dma_start(ints[:, 2, :], type_cols).then_inc(edges_here, 16)
            sp.dma_start(units_i[:, :], dst_units).then_inc(edges_here, 16)
            sp.dma_start(xT_raw[:, :, :], xT.rearrange("(k p) n -> p k n", p=P)).then_inc(xT_here, 16)
            for k in range(RING):
                load_chunk(0, k, first=True)
            sp.wait_ge(turned_read, WINDOWS + 2)
            for m in range(NT):
                sp.dma_start(counts_dram[:, m, :, :].rearrange("r p n -> p r n"), counts[:, m, :, :]).then_inc(flushed, 16)
            sp.wait_ge(summed, 1)
            sp.dma_start(a_bc[:, :], a[0, :].partition_broadcast(P)).then_inc(a_here, 16)
            load_ahead(0)
            load_ahead(1)
            sp.wait_ge(attT_lo_done, NT)
            sp.wait_ge(flushed, 16 * NT)
            sp.dma_start(u[:, 0:NT - 1, :], x[0:P * (NT - 1), :].rearrange("(t p) d -> p t d", p=P)).then_inc(x_here, 16)
            sp.dma_start(u[0:rows(NT - 1), NT - 1, :], x[P * (NT - 1):N, :]).then_inc(x_here, 16)
            sp.dma_start(bias_bc[:, :], bias.partition_broadcast(P)).then_inc(bias_here, 16)
            sp.dma_start(bg_bc[:, :], b_gate.partition_broadcast(P)).then_inc(bias_here, 16)
            sp.dma_start(c16[:, :, :], counts_dram[0, :, :, :].rearrange("m p n -> p m n")).then_inc(c16_here, 16)

            def step_loads(i, last):
                for h in range(2):
                    n = 2 * i + SEG_U + h
                    for k in range(KT - RING):
                        load_chunk(n, k + RING, at=((i + 1) * D + (k + RING) * P, h * H2))
                    for k in range(RING):
                        load_chunk(n + 1, k, at=((i + 1 + h) * D + k * P, (1 - h) * H2))
                if not last:
                    sp.wait_ge(C_ready, i + 1)
                    sp.dma_start(c16[:, :, :], counts_dram[ds(i + 1, 1), :, :, :].rearrange("o m p n -> p (o m) n"))\
                      .then_inc(c16_here, 16)

            with sp.Fori(0, R // 2 - 1) as j:
                for s in range(2):
                    step_loads(2 * j + s, False)
            step_loads(R - 2, False)
            step_loads(R - 1, True)
            for n in range(SEG_U + 2 * R, SEGS):
                load_ahead(n, last=n == SEGS - 1)
            for t in range(NT):
                sp.wait_ge(y2_done, t + 1)
                sp.dma_start(out[t * P:t * P + rows(t), :], u[0:rows(t), t, :]).then_inc(out_done, 16)
            sp.wait_ge(out_done, 16 * NT)

        @block.gpsimd
        def _(pool):
            steps = [0]

            def step(ins):
                steps[0] += 1
                ins.then_inc(pool_step, 1)
                pool.wait_ge(pool_step, steps[0])

            pool.sem_inc(m_lo_done, 4)
            pool.iota(iota_i[:, :], pattern=[[1, NP]], base=0, channel_multiplier=0).then_inc(pool_consts, 1)
            pool.iota(part_col[:, :], pattern=[[0, 1]], base=0, channel_multiplier=1,
                      allow_small_or_imprecise_dtypes=True).then_inc(pool_consts, 1)
            pool.iota(iota_up[:, :], pattern=[[1, UNITS]], base=1, channel_multiplier=0,
                      allow_small_or_imprecise_dtypes=True).then_inc(pool_consts, 1)
            pool.iota(iota_down[:, :], pattern=[[-1, UNITS]], base=1000, channel_multiplier=0,
                      allow_small_or_imprecise_dtypes=True).then_inc(pool_consts, 1)
            pool.iota(win_base[:, :], pattern=[[P, WINDOWS]], base=0, channel_multiplier=0,
                      allow_small_or_imprecise_dtypes=True).then_inc(pool_consts, 1)

            def split_chunk(n, k):
                pool.wait_ge(w_hi_done, 8 * n + k + 1)
                pool.tensor_tensor(w_lo[k % RING][:, :], w_raw[k % RING][:, :], w_hi[k % RING][:, :].bitcast(f32),
                                   ALU.subtract).then_inc(w_lo_done, 1)

            def split_ahead(n, last=False):
                for k in range(KT):
                    if k < KT - RING:
                        split_chunk(n, k + RING)
                    elif not last:
                        split_chunk(n + 1, k + RING - KT)

            for k in range(RING):
                split_chunk(0, k)
            pool.wait_ge(xT_hi_done, 1)
            pool.tensor_tensor(M_lo[0][:, :, 0:N], xT_raw[:, :, :], M_hi[0][:, :, 0:N].bitcast(f32),
                               ALU.subtract).then_inc(xT_lo_done, 1)
            split_ahead(0)
            split_ahead(1)
            for t in range(NT):
                pool.wait_ge(x1_hi_done, t + 1)
                pool.tensor_tensor(x1_lo[0:rows(t), t, :], u[0:rows(t), t, :], x1_hi[0:rows(t), t, :].bitcast(f32),
                                   ALU.subtract).then_inc(x1_lo_done, 1)

            def means(i, odd, half):
                for e in range(half * MEANS // 2, (half + 1) * MEANS // 2):
                    c0, cn = NCOL[e % 2]
                    pool.wait_ge(m_hi_done, MEANS * i + e + 1)
                    pool.tensor_tensor(M_lo[1 - odd][:, e // 2, c0:c0 + cn], mt[e % 4][:, 0:cn],
                                       M_hi[1 - odd][:, e // 2, c0:c0 + cn].bitcast(f32), ALU.subtract)\
                        .then_inc(m_lo_done, 1)

            def step_work(i, odd):
                for half in range(2):
                    split_ahead(2 * i + SEG_U + half)
                    means(i, odd, half)

            with pool.Fori(0, R // 2) as j:
                for s in range(2):
                    step_work(2 * j + s, s)
            split_ahead(SEG_U + 2 * R)
            split_ahead(SEG_U + 2 * R + 1)
            split_ahead(SEG_G)
            for t in range(NT):
                r = slice(0, rows(t))
                if t == 0:
                    pool.wait_ge(g_drained, 3 + ITEMS * R)
                pool.tensor_tensor(xf[r, t, :], x1_hi[r, t, :].bitcast(f32), x1_lo[r, t, :].bitcast(f32), ALU.add)\
                    .then_inc(xf_done, 1)
            split_ahead(SEG_G + 1)
            for t in range(NT):
                r = slice(0, rows(t))
                pool.wait_ge(tanh_done, t + 1)
                pool.wait_ge(xf_done, t + 1)
                pool.tensor_tensor(u[r, t, :], u[r, t, :], xf[r, t, :], ALU.subtract).then_inc(d_done, 1)
            split_ahead(SEG_G + 2)
            split_ahead(SEG_G + 3, last=True)

        @block.scalar
        def _(act):
            act.sem_inc(window_copied, 2)
            act.sem_inc(turned_read, 2)

            def split_chunk(n, k, first=False):
                act.wait_ge(raw_here[k % RING], 32 * n + 16 * (k // RING) + 16)
                if not first:
                    m, j = (n, k - RING) if k >= RING else (n - 1, k + KT - RING)
                    if closes(m) and j == KT - 1:
                        act.wait_ge(u_ready, filled(m))
                    else:
                        act.wait_ge(w_used, used_before(m) + j + 1)
                nc.scalar.copy(w_hi[k % RING][:, :], w_raw[k % RING][:, :]).then_inc(w_hi_done, 1)

            def split_ahead(n, last=False):
                for k in range(KT):
                    if k < KT - RING:
                        split_chunk(n, k + RING)
                    elif not last:
                        split_chunk(n + 1, k + RING - KT)

            for k in range(RING):
                split_chunk(0, k, first=True)
            act.wait_ge(xT_here, 16)
            nc.scalar.copy(M_hi[0][:, :, 0:N], xT_raw[:, :, :]).then_inc(xT_hi_done, 1)

            with act.Fori(0, NT) as g:
                for w8 in range(GROUP):
                    act.wait_ge(window_counted, GROUP * g + w8 + 1)
                    b = w8 % 2
                    nc.scalar.copy(win_sb[b][:, :].rearrange("p (b n) -> p b n", b=2),
                                   pair(b).rearrange("p (b n) -> p b n", b=2)[:, :, 0:SPLIT]).then_inc(window_copied, 1)
                    for v8 in ([w8 - 1] if w8 else []) + ([w8] if w8 == GROUP - 1 else []):
                        act.wait_ge(turned, GROUP * g + v8 + 1)
                        nc.scalar.copy(counts[:, :, :, ds(P * g + WIN * v8, WIN)],
                                       pair(2 + v8 % 2)[:, 0:NP].rearrange("p (m d r) -> p m r d", m=NT, r=R))\
                          .then_inc(turned_read, 1)

            for half in range(2):
                split_ahead(half)
                for t in range(NT):
                    act.wait_ge(u_ready, NT * half + t + 1)
                    nc.scalar.copy(h_hi[0:rows(t), t, half * H2:(half + 1) * H2], bank(t, rows(t))).then_inc(h_hi_done, 1)
            act.wait_ge(ar_bcast, 1)
            act.wait_ge(diag_done, 1)
            for t in range(NT):
                nc.scalar.activation(att[0:rows(t), t, :].rearrange("p (b n) -> p b n", b=2),
                                     ps[0:rows(t), 5 * H2:7 * H2].rearrange("p (b n) -> p b n", b=2)[:, :, 0:SPLIT],
                                     ACT.Identity, bias=alr[0:rows(t), t:t + 1]).then_inc(sum_done, 1)
            for t in range(NT):
                act.wait_ge(leaky_done, t + 1)
                nc.scalar.activation(att[0:rows(t), t, :], att[0:rows(t), t, :], ACT.Exp, scale=-1.0).then_inc(exp_done, 1)
            for t in range(NT):
                act.wait_ge(attT_ready, t + 1)
                nc.scalar.copy(M_hi[0][0:rows(t), t, 0:N], pair(t % 3, rows(t))[:, 0:N]).then_inc(attT_hi_done, 1)
            for t in range(NT):
                act.wait_ge(elu_in, t + 1)
                nc.scalar.activation(et[t % 2][0:rows(t), :], et[t % 2][0:rows(t), :], ACT.Exp).then_inc(elu_exp, 1)
            act.wait_ge(y_done, NT)
            nc.scalar.activation(rstd[:, :], mv[:, :, 1], ACT.Sqrt, bias=eps_col[:, :]).then_inc(std_done, 1)
            for t in range(NT):
                act.wait_ge(x1_done, t + 1)
                nc.scalar.copy(x1_hi[0:rows(t), t, :], u[0:rows(t), t, :]).then_inc(x1_hi_done, 1)
                act.wait_ge(x1T_ready, t + 1)
                nc.scalar.copy(M_hi[0][:, :, t * P:t * P + rows(t)],
                               pair(t % 3).rearrange("p (k n) -> p k n", k=KT)[:, :, 0:rows(t)]).then_inc(x1T_hi_done, 1)

            def means(i, odd, half):
                for e in range(half * MEANS // 2, (half + 1) * MEANS // 2):
                    c0, cn = NCOL[e % 2]
                    act.wait_ge(g_drained, ITEMS * i + e + 2 + 3 + 1)
                    nc.scalar.copy(M_hi[1 - odd][:, e // 2, c0:c0 + cn], mt[e % 4][:, 0:cn]).then_inc(m_hi_done, 1)

            def step_work(i, odd):
                for half in range(2):
                    split_ahead(2 * i + SEG_U + half)
                    means(i, odd, half)

            with act.Fori(0, R // 2) as j:
                for s in range(2):
                    step_work(2 * j + s, s)

            for half in range(2):
                split_ahead(SEG_U + 2 * R + half)
                for t, kh in [(t, kh) for t in range(NT) for kh in range(2)][half * NT:(half + 1) * NT]:
                    act.wait_ge(xt2_ready, 2 * (2 * t + kh) + 1)
                    nc.scalar.copy(M_hi[1][:, 4 * kh:4 * kh + 4, t * P:t * P + rows(t)],
                                   bank(5 + 2 * (2 * t + kh) % GB).rearrange("p (k n) -> p k n", k=4)[:, :, 0:rows(t)])\
                      .then_inc(xt2_hi_done, 1)
            split_ahead(SEG_G)
            for t in range(NT):
                for kh in range(2):
                    it = 2 * t + kh
                    act.wait_ge(uT_ready, it + 1)
                    nc.scalar.copy(M_hi[0][:, 4 * kh:4 * kh + 4, t * P:t * P + rows(t)],
                                   bank(5 + it % GB).rearrange("p (k n) -> p k n", k=4)[:, :, 0:rows(t)])\
                      .then_inc(uT_hi_done, 1)
            split_ahead(SEG_G + 1)
            for t in range(NT):
                nc.scalar.activation(u[0:rows(t), t, :], u[0:rows(t), t, :], ACT.Tanh).then_inc(tanh_done, 1)
            split_ahead(SEG_G + 2)
            split_ahead(SEG_G + 3, last=True)
            for t in range(NT):
                act.wait_ge(var_done, t + 1)
                nc.scalar.activation(rstd[0:rows(t), t:t + 1], mv[0:rows(t), t, 1:2], ACT.Sqrt,
                                     bias=eps_col[0:rows(t), :]).then_inc(std2_done, 1)

        @block.vector
        def _(dve):
            steps = [0]

            def step(ins):
                steps[0] += 1
                ins.then_inc(dve_step, 1)
                dve.wait_ge(dve_step, steps[0])

            v = nc.vector
            dve.sem_inc(g_drained, 3)
            v.memset(ones[:, :], 1.0)
            v.memset(zeros[:, :], 0.0)
            v.memset(ones_r[:, :].bitcast(f32), 1.0)
            v.memset(eps_col[:, :], EPS)
            v.memset(rowsum[:, :], 1.0)
            v.memset(mv[:, :, :], 1.0)
            step(v.memset(dots[:, :, :], 0.0))
            dve.wait_ge(pool_consts, 5)
            step(v.tensor_copy(iota_node[:, :], iota_i[:, :]))
            step(v.tensor_scalar(ident[:, :], iota_node[:, 0:P], part_col[:, :], None, ALU.is_equal))
            v.tensor_scalar(win_edge[:, 0:1], part_col[:, :], float(WIN), None, ALU.mult)
            step(v.tensor_scalar(win_edge[:, 1:2], part_col[:, :], float(WIN), float(WIN - 1), ALU.mult, ALU.add))
            dve.wait_ge(edges_here, 64)
            v.tensor_reduce(unit_mm[:, 0:1], units_i[:, :], X, ALU.max)
            step(v.tensor_reduce(unit_mm[:, 1:2], units_i[:, :], X, ALU.min))
            for c in range(2):
                d = v.tensor_scalar(unit_diag[:, c, 0:UNITS], ident[0:UNITS, 0:UNITS], unit_mm[:, c:c + 1], None, ALU.mult)
            d.then_inc(units_diag_done, 1)
            v.tensor_copy(src_f[:, :], ints[:, 1, :])
            step(v.tensor_copy(q_f[:, :], ints[:, 0, :]))
            step(v.tensor_copy(type_f[:, :], ints[:, 2, :]))
            step(v.scalar_tensor_tensor(q_f[:, :], q_f[:, :], float(R), type_f[:, :], ALU.mult, ALU.add))
            dve.wait_ge(units_bcast, 1)
            step(v.scalar_tensor_tensor(reach[:, 0, :], ps[0:WINDOWS, 4 * H2:4 * H2 + UNITS], win_edge[0:WINDOWS, 0:1],
                                        iota_down[0:WINDOWS, :], ALU.is_ge, ALU.mult))
            step(v.scalar_tensor_tensor(reach[:, 1, :], ps[0:WINDOWS, 5 * H2:5 * H2 + UNITS], win_edge[0:WINDOWS, 1:2],
                                        iota_up[0:WINDOWS, :], ALU.is_le, ALU.mult))
            step(v.tensor_reduce(lohi[:, 0:2], reach[:, :, :], X, ALU.max))
            step(v.tensor_scalar(lohi[:, 2:3], lohi[:, 0:1], -1.0, 1000.0, ALU.mult, ALU.add))
            v.tensor_scalar(lohi[:, 3:4], lohi[:, 2:3], 1.0, lohi[:, 1:2], ALU.add, ALU.max).then_inc(lohi_done, 1)
            dve.wait_ge(lohi_turned, 1)
            v.tensor_copy(lohi_row[:, 0:WINDOWS], ps[0:1, 6 * H2:6 * H2 + WINDOWS])
            v.tensor_copy(lohi_row[:, WINDOWS:2 * WINDOWS], ps[0:1, 7 * H2:7 * H2 + WINDOWS]).then_inc(row_done, 1)
            dve.wait_ge(row_done, 1)

            turn = dve.alloc_register("dve_turn")
            dve.reg_mov(turn, 0)
            with dve.Fori(0, NT) as g:
                for w8 in range(GROUP):
                    w = g * GROUP + w8
                    lo = dve.value_load(lohi_row[0:1, ds(w, 1)], min_val=0, max_val=UNITS - 1)
                    hi = dve.value_load(lohi_row[0:1, ds(w + WINDOWS, 1)], min_val=1, max_val=UNITS)
                    with dve.Fori(lo, hi) as unit:
                        dve.reg_add(turn, turn, 1)
                        n = dve.snap(turn, min_val=1, max_val=WINDOWS * UNITS)
                        for s in range(PAIR):
                            col = ds(unit * PAIR + s, 1)
                            dve.wait_ge(slot_free[s], n)
                            v.tensor_scalar(hot_src[s][:, :], iota_node[:, :], src_f[:, col], None, ALU.is_equal)
                            v.tensor_scalar(hot_q[s][:, :], iota_node[:, 0:P], win_base[:, ds(w, 1)], q_f[:, col],
                                            ALU.add, ALU.is_equal).then_inc(built[s], 1)

            dve.wait_ge(xT_lo_done, 1)
            dve.wait_ge(turned_read, WINDOWS + 2)
            step(v.tensor_tensor(sums[:, :, :, :], counts[:, :, 0:R // 2, :], counts[:, :, R // 2:R, :], ALU.add))
            step(v.tensor_tensor(sums[:, :, 0:R // 4, :], sums[:, :, 0:R // 4, :], sums[:, :, R // 4:R // 2, :], ALU.add))
            v.tensor_tensor(counts_all[:, :, :], sums[:, :, 0, :], sums[:, :, 1, :], ALU.add).then_inc(summed, 1)
            dve.wait_ge(a_here, 16)
            for half in range(2):
                for t in range(NT):
                    r = slice(0, rows(t))
                    dve.wait_ge(h_hi_done, NT * half + t + 1)
                    v.tensor_tensor(h_lo[r, t, half * H2:(half + 1) * H2], bank(t, rows(t)),
                                    h_hi[r, t, half * H2:(half + 1) * H2].bitcast(f32), ALU.subtract)
                    for lr in range(2):
                        c0 = lr * D + half * H2
                        d = v.tensor_tensor_reduce(out=junk[r, :], in0=bank(t, rows(t)), in1=a_bc[r, c0:c0 + H2],
                                                   scale=1.0, scalar=0.0, op0=ALU.mult, op1=ALU.add,
                                                   accum_out=dots[r, half, lr * NT + t:lr * NT + t + 1])
                        if lr == 0:
                            step(d)
                    d.then_inc(u_drained, 1)
                    dve.wait_ge(u_drained, NT * half + t + 1)
            step(v.tensor_tensor(alr[:, :], dots[:, 0, :], dots[:, 1, :], ALU.add))
            for t in range(NT):
                d = v.tensor_scalar(diag[:, t, :], ident[:, :], alr[:, NT + t:NT + t + 1], None, ALU.mult)
            d.then_inc(diag_done, 1)
            for t in range(NT):
                r = slice(0, rows(t))
                dve.wait_ge(sum_done, t + 1)
                v.scalar_tensor_tensor(att[r, t, :], att[r, t, :], SLOPE, att[r, t, :], ALU.mult, ALU.max)\
                    .then_inc(leaky_done, 1)
            for t in range(NT):
                r = slice(0, rows(t))
                dve.wait_ge(exp_done, t + 1)
                v.scalar_tensor_tensor(att[r, t, :], att[r, t, :], FLT_MAX, counts_all[r, t, :], ALU.min, ALU.mult,
                                       accum_out=rowsum[r, t:t + 1]).then_inc(att_done, 1)
            dve.wait_ge(att_done, NT)
            step(v.tensor_scalar(rowsum[:, :], rowsum[:, :], EPS, None, ALU.add))
            step(v.reciprocal(rowsum[:, :], rowsum[:, :]))
            for t in range(NT):
                r = slice(0, rows(t))
                dve.wait_ge(attT_hi_done, t + 1)
                v.tensor_tensor(M_lo[0][r, t, 0:N], pair(t % 3, rows(t))[:, 0:N], M_hi[0][r, t, 0:N].bitcast(f32),
                                ALU.subtract).then_inc(attT_lo_done, 1)
            dve.wait_ge(x_here, 32)

            def elu_start(t):
                r = slice(0, rows(t))
                dve.wait_ge(hp_ready, t + 1)
                v.tensor_scalar(et[t % 2][r, :], pair(t % 3, rows(t)), rowsum[r, t:t + 1], 0.0, ALU.mult, ALU.min)\
                    .then_inc(elu_in, 1)
                v.tensor_scalar(gt[t % 2][r, :], pair(t % 3, rows(t)), rowsum[r, t:t + 1], 0.0, ALU.mult, ALU.max)\
                    .then_inc(hp_read, 1)

            def elu_end(t):
                r = slice(0, rows(t))
                dve.wait_ge(elu_exp, t + 1)
                dve.wait_ge(hp_read, t + 1)
                step(v.scalar_tensor_tensor(gt[t % 2][r, :], et[t % 2][r, :], -1.0, gt[t % 2][r, :], ALU.add, ALU.add))
                step(v.tensor_tensor(u[r, t, :], gt[t % 2][r, :], u[r, t, :], ALU.add))
                for c in range(2):
                    s_ = v.bn_stats(stats[r, t % 2, c, :], u[r, t, c * H2:(c + 1) * H2])
                step(s_)
                v.bn_aggr(mv[r, t, :], stats[r, t % 2, :, :]).then_inc(y_done, 1)

            for t in range(NT):
                elu_start(t)
                if t:
                    elu_end(t - 1)
            elu_end(NT - 1)
            dve.wait_ge(std_done, 1)
            step(v.reciprocal(rstd[:, :], rstd[:, :]))
            for t in range(NT):
                r = slice(0, rows(t))
                v.tensor_scalar(u[r, t, :], u[r, t, :], mv[r, t, 0:1], rstd[r, t:t + 1], ALU.subtract, ALU.mult)\
                    .then_inc(x1_done, 1)
            for t in range(NT):
                dve.wait_ge(x1T_hi_done, t + 1)
                v.tensor_tensor(M_lo[0][:, :, t * P:t * P + rows(t)],
                                pair(t % 3).rearrange("p (k n) -> p k n", k=KT)[:, :, 0:rows(t)],
                                M_hi[0][:, :, t * P:t * P + rows(t)].bitcast(f32), ALU.subtract).then_inc(x1T_lo_done, 1)
            dve.wait_ge(x1_lo_done, NT)
            dve.wait_ge(bias_here, 32)
            for t in range(NT):
                d = v.tensor_copy(u[:, t, :], bias_bc[:, :])
            d.then_inc(u_init, 1)
            dve.wait_ge(u_init, 1)

            def convert_counts(i):
                dve.wait_ge(c16_here, 16 * i + 16)
                v.tensor_copy(C_hi[:, :, :], c16[:, :, :]).then_inc(C_ready, 1)

            def add_u(i, half, t):
                r = slice(0, rows(t))
                dve.wait_ge(u_ready, 2 * NT * i + NT * (SEG_U + half) + t + 1)
                v.tensor_tensor(u[r, t, half * H2:(half + 1) * H2], bank(t, rows(t)), u[r, t, half * H2:(half + 1) * H2],
                                ALU.add).then_inc(u_drained, 1)

            def invert(i, q):
                c0, cn = NCOL[q]
                dve.wait_ge(g_ready, ITEMS * i + q + 1)
                v.tensor_scalar(inv[:, c0:c0 + cn], bank(5 + q, c=cn), 1.0, None, ALU.max).then_inc(g_drained, 1)
                dve.wait_ge(g_drained, ITEMS * i + 3 + q + 1)
                v.reciprocal(inv[:, c0:c0 + cn], inv[:, c0:c0 + cn]).then_inc(inv_ready, 1)

            def scale_mean(i, e):
                q = e + 2
                c0, cn = NCOL[e % 2]
                if e == 0:
                    dve.wait_ge(inv_ready, 2 * i + 2)
                dve.wait_ge(g_ready, ITEMS * i + q + 1)
                dve.wait_ge(m_lo_done, MEANS * i + e + 1)
                v.tensor_tensor(mt[e % 4][:, 0:cn], bank(5 + q % GB, c=cn), inv[:, c0:c0 + cn], ALU.mult)\
                    .then_inc(g_drained, 1)

            def step_work(i):
                convert_counts(i)
                for half in range(2):
                    add_u(i, half, 0)
                    if half == 0:
                        invert(i, 0)
                        invert(i, 1)
                    for n in range(MEANS // 2):
                        scale_mean(i, half * MEANS // 2 + n)
                        if n < NT - 1:
                            add_u(i, half, n + 1)

            with dve.Fori(0, R // 2) as j:
                for s in range(2):
                    step_work(2 * j + s)

            for half in range(2):
                for t in range(NT):
                    add_u(R, half, t)
                for t, kh in [(t, kh) for t in range(NT) for kh in range(2)][half * NT:(half + 1) * NT]:
                    it = 2 * (2 * t + kh) + 1
                    dve.wait_ge(xt2_ready, it + 1)
                    v.tensor_copy(M_lo[1][:, 4 * kh:4 * kh + 4, t * P:t * P + rows(t)],
                                  bank(5 + it % GB).rearrange("p (k n) -> p k n", k=4)[:, :, 0:rows(t)])\
                        .then_inc(xt2_lo_done, 1)
            for t in range(NT):
                for kh in range(2):
                    it = 2 * t + kh
                    dve.wait_ge(uT_hi_done, it + 1)
                    v.tensor_tensor(M_lo[0][:, 4 * kh:4 * kh + 4, t * P:t * P + rows(t)],
                                    bank(5 + it % GB).rearrange("p (k n) -> p k n", k=4)[:, :, 0:rows(t)],
                                    M_hi[0][:, 4 * kh:4 * kh + 4, t * P:t * P + rows(t)].bitcast(f32), ALU.subtract)\
                        .then_inc(uT_lo_done, 1)
            for half in range(2):
                for t in range(NT):
                    r, c = slice(0, rows(t)), slice(half * H2, (half + 1) * H2)
                    z = zt[t % 2]
                    dve.wait_ge(u_ready, BANKS_G + NT * half + t + 1)
                    v.tensor_tensor(z[r, :], bank(t, rows(t)), bg_bc[r, c], ALU.add).then_inc(u_drained, 1)
                    dve.wait_ge(u_drained, BANKS_G + NT * half + t + 1)
                    dve.wait_ge(d_done, t + 1)
                    step(v.tensor_tensor(z[r, :], z[r, :], u[r, t, c], ALU.mult))
                    step(v.scalar_tensor_tensor(u[r, t, c], xf[r, t, c], 2.0, z[r, :], ALU.mult, ALU.add))
                    if half:
                        for hh in range(2):
                            s_ = v.bn_stats(stats[r, t % 2, hh, :], u[r, t, hh * H2:(hh + 1) * H2])
                        step(s_)
                        v.bn_aggr(mv[r, t, :], stats[r, t % 2, :, :]).then_inc(var_done, 1)
            for t in range(NT):
                r = slice(0, rows(t))
                dve.wait_ge(std2_done, t + 1)
                step(v.reciprocal(rstd[r, t:t + 1], rstd[r, t:t + 1]))
                v.tensor_scalar(u[r, t, :], u[r, t, :], mv[r, t, 0:1], rstd[r, t:t + 1], ALU.subtract, ALU.mult)\
                    .then_inc(y2_done, 1)

        @block.tensor
        def _(pe):
            mm = nc.tensor.matmul
            for s in range(PAIR):
                pe.sem_inc(slot_free[s], 1)

            pe.wait_ge(units_diag_done, 1)
            for c in range(2):
                last = mm(ps[0:WINDOWS, (4 + c) * H2:(4 + c) * H2 + UNITS], ones[0:UNITS, 0:WINDOWS],
                          unit_diag[:, c, 0:UNITS], start=True, stop=True)
            last.then_inc(units_bcast, 1)
            pe.wait_ge(lohi_done, 1)
            for c in range(2):
                last = mm(ps[0:1, (6 + c) * H2:(6 + c) * H2 + WINDOWS], lohi[:, 2 + c:3 + c],
                          ident[0:WINDOWS, 0:WINDOWS], start=True, stop=True)
            last.then_inc(lohi_turned, 1)

            pe.wait_ge(row_done, 1)
            turn = pe.alloc_register("pe_turn")
            pe.reg_mov(turn, 0)
            with pe.Fori(0, NT) as g:
                for w8 in range(GROUP):
                    w = g * GROUP + w8
                    lo = pe.value_load(lohi_row[0:1, ds(w, 1)], min_val=0, max_val=UNITS - 1)
                    hi = pe.value_load(lohi_row[0:1, ds(w + WINDOWS, 1)], min_val=1, max_val=UNITS)
                    b = w8 % 2
                    pe.wait_ge(window_copied, w + 1)
                    for c in range(2):
                        mm(bank(2 * b + c, c=2), zeros[:, :], zeros[:, 0:2], start=True, stop=False, skip_group_check=True)
                    with pe.Fori(lo, hi) as unit:
                        pe.reg_add(turn, turn, 1)
                        n = pe.snap(turn, min_val=1, max_val=WINDOWS * UNITS)
                        for s in range(PAIR):
                            pe.wait_ge(built[s], n)
                            for c in range(2):
                                last = mm(bank(2 * b + c, c=SPLIT), hot_q[s][:, :], hot_src[s][:, c * SPLIT:(c + 1) * SPLIT],
                                          start=False, stop=False, skip_group_check=True)
                            last.then_inc(slot_free[s], 1)
                    for c in range(2):
                        last = mm(bank(2 * b + c, c=2), zeros[:, :], zeros[:, 0:2], start=False, stop=True,
                                  skip_group_check=True)
                    last.then_inc(window_counted, 1)
                    for v8 in ([w8 - 1] if w8 else []) + ([w8] if w8 == GROUP - 1 else []):
                        pe.wait_ge(window_copied, g * GROUP + v8 + 3)
                        pe.wait_ge(turned_read, g * GROUP + v8 + 1)
                        for m in range(NT):
                            last = nc.tensor.transpose(pair(2 + v8 % 2)[:, m * P:(m + 1) * P],
                                                       win_sb[v8 % 2][:, m * P:(m + 1) * P], ident[:, :])
                        last.then_inc(turned, 1)

            def product(n, lhs_hi, lhs_lo, before, open_=True, close=True):
                for k in range(KT):
                    pe.wait_ge(w_lo_done, 8 * n + k + 1)
                    for t in range(NT):
                        if k == 0 and open_ and before is not None:
                            pe.wait_ge(u_drained, before - NT + t + 1)
                        c = slice(t * P, t * P + rows(t))
                        o = bank(t, rows(t))
                        mm(o, lhs_hi[:, k, c], w_hi[k % RING][:, :], start=open_ and k == 0, stop=False)
                        mm(o, lhs_lo[:, k, c], w_hi[k % RING][:, :], start=False, stop=False)
                        last = mm(o, lhs_hi[:, k, c], w_lo[k % RING][:, :], start=False, stop=close and k == KT - 1)
                        if close and k == KT - 1:
                            last.then_inc(u_ready, 1)
                        elif t == NT - 1:
                            last.then_inc(w_used, 1)

            pe.wait_ge(xT_lo_done, 1)
            pe.wait_ge(turned_read, WINDOWS + 2)
            product(0, M_hi[0], M_lo[0], None)
            product(1, M_hi[0], M_lo[0], NT)
            pe.wait_ge(diag_done, 1)
            for c in range(2):
                last = mm(bank(5 + c, c=SPLIT), ones[:, :], diag[:, :, :].rearrange("p a b -> p (a b)")[:, c * SPLIT:(c + 1) * SPLIT],
                          start=True, stop=True)
            last.then_inc(ar_bcast, 1)
            pe.wait_ge(att_done, NT)
            for d in range(NT):
                if d >= 3:
                    pe.wait_ge(attT_lo_done, d - 2)
                for t in range(NT):
                    last = nc.tensor.transpose(pair(d % 3)[:, t * P:t * P + rows(t)], att[0:rows(t), t, d * P:(d + 1) * P],
                                               ident[0:rows(t), 0:rows(t)])
                last.then_inc(attT_ready, 1)
            pe.wait_ge(attT_lo_done, NT)
            for t in range(NT):
                if t >= 3:
                    pe.wait_ge(hp_read, t - 2)
                c = slice(t * P, t * P + rows(t))
                for half in range(2):
                    o = bank(2 * (t % 3) + half, rows(t))
                    hc = slice(half * H2, (half + 1) * H2)
                    for d in range(NT):
                        k = slice(0, rows(d))
                        mm(o, M_hi[0][k, d, c], h_hi[k, d, hc], start=d == 0, stop=False)
                        mm(o, M_lo[0][k, d, c], h_hi[k, d, hc], start=False, stop=False)
                        last = mm(o, M_hi[0][k, d, c], h_lo[k, d, hc], start=False, stop=d == NT - 1)
                last.then_inc(hp_ready, 1)
            for t in range(NT):
                pe.wait_ge(x1_done, t + 1)
                if t >= 3:
                    pe.wait_ge(x1T_lo_done, t - 2)
                for k in range(KT):
                    last = nc.tensor.transpose(pair(t % 3)[:, k * P:k * P + rows(t)], u[0:rows(t), t, k * P:(k + 1) * P],
                                               ident[0:rows(t), 0:rows(t)])
                last.then_inc(x1T_ready, 1)
            pe.wait_ge(x1T_lo_done, NT)

            def aggregate(i, half):
                if half == 0:
                    pe.wait_ge(C_ready, i + 1)
                for q in range(0 if half == 0 else 2 + MEANS // 2, 2 + (half + 1) * MEANS // 2):
                    c0, cn = NCOL[q % 2]
                    o = bank(5 + q % GB, c=cn)
                    pe.wait_ge(g_drained, ITEMS * i + q + 1)
                    for m in range(NT):
                        if q < 2:
                            last = mm(o, ones_r[:, :], C_hi[:, m, c0:c0 + cn], start=m == 0, stop=m == NT - 1)
                        else:
                            r, f = slice(0, rows(m)), slice((q - 2) // 2 * P, (q - 2) // 2 * P + P)
                            mm(o, x1_hi[r, m, f], C_hi[r, m, c0:c0 + cn], start=m == 0, stop=False)
                            last = mm(o, x1_lo[r, m, f], C_hi[r, m, c0:c0 + cn], start=False, stop=m == NT - 1)
                    last.then_inc(g_ready, 1)

            def step_work(i, odd):
                for half in range(2):
                    n = 2 * i + SEG_U + half
                    product(n, M_hi[odd], M_lo[odd], 2 * NT * i + NT * (SEG_U + half))
                    aggregate(i, half)
                pe.wait_ge(m_lo_done, MEANS * i + MEANS + 4)

            with pe.Fori(0, R // 2) as j:
                for s in range(2):
                    step_work(2 * j + s, s)
            for half in range(2):
                n = SEG_U + 2 * R + half
                product(n, M_hi[0], M_lo[0], NT * n)
                for t, kh in [(t, kh) for t in range(NT) for kh in range(2)][half * NT:(half + 1) * NT]:
                    for lo_, src in enumerate((x1_hi, x1_lo)):
                        it = 2 * (2 * t + kh) + lo_
                        if it >= GB:
                            b4 = it - GB
                            pe.wait_ge(xt2_lo_done if b4 % 2 else xt2_hi_done, b4 // 2 + 1)
                        elif it == 0:
                            pe.wait_ge(g_drained, ITEMS * R + 3)
                        for k in range(4):
                            f = slice((4 * kh + k) * P, (4 * kh + k + 1) * P)
                            last = nc.tensor.transpose(bank(5 + it % GB, c0=k * P, c=rows(t)),
                                                       src[0:rows(t), t, f].bitcast(f32), ident[0:rows(t), 0:rows(t)])
                        last.then_inc(xt2_ready, 1)
            pe.wait_ge(xt2_lo_done, 2 * NT)
            pe.wait_ge(xt2_hi_done, 2 * NT)
            product(SEG_G, M_hi[1], M_lo[1], BANKS_G, close=False)
            for t in range(NT):
                for kh in range(2):
                    it = 2 * t + kh
                    if it >= GB:
                        pe.wait_ge(uT_lo_done, it - GB + 1)
                    for k in range(4):
                        last = nc.tensor.transpose(bank(5 + it % GB, c0=k * P, c=rows(t)),
                                                   u[0:rows(t), t, (4 * kh + k) * P:(4 * kh + k + 1) * P],
                                                   ident[0:rows(t), 0:rows(t)])
                    last.then_inc(uT_ready, 1)
            pe.wait_ge(uT_lo_done, 2 * NT)
            product(SEG_G + 1, M_hi[0], M_lo[0], None, open_=False)
            product(SEG_G + 2, M_hi[1], M_lo[1], BANKS_G + NT, close=False)
            product(SEG_G + 3, M_hi[0], M_lo[0], None, open_=False)


def kernel(**inputs):
    import numpy as np
    import concourse.bacc as bacc
    from concourse import mybir
    from concourse.bass_utils import run_bass_kernel_spmd

    x = np.ascontiguousarray(inputs["x"])
    n, d = x.shape
    relations = inputs["L1_gnn_weight"].shape[0]
    edges = inputs["dst"].shape[0]
    tiles = 2 * -(-edges // 256)
    far = 1 << 20

    def padded(v, fill):
        row = np.full((tiles * 128,), fill, np.int32)
        row[:edges] = v
        return row

    dst = padded(inputs["dst"], far)
    w_gate = np.asarray(inputs["L1_gnn_w_gate"])
    arrays = {
        "dst_cols": np.ascontiguousarray(dst.reshape(tiles, 128).T),
        "src_cols": np.ascontiguousarray(padded(inputs["src"], 0).reshape(tiles, 128).T),
        "type_cols": np.ascontiguousarray(padded(inputs["edge_type_8"], 0).reshape(tiles, 128).T),
        "dst_units": dst.reshape(tiles // 2, 256),
        "xT": np.ascontiguousarray(x.T),
        "x": x,
        "weights": np.concatenate([np.asarray(inputs["L0_gnn_W"]), np.asarray(inputs["L1_gnn_root"]),
                                   np.asarray(inputs["L1_gnn_weight"]).reshape(relations * d, d), w_gate]),
        "a": np.ascontiguousarray(inputs["L0_gnn_a"]),
        "bias": np.ascontiguousarray(inputs["L1_gnn_bias"]),
        "b_gate": np.ascontiguousarray(inputs["L1_gnn_b_gate"]),
    }
    nc = bacc.Bacc("TRN2", target_bir_lowering=False, num_devices=1)
    args = [nc.dram_tensor(name, v.shape, mybir.dt.from_np(v.dtype), kind="ExternalInput").ap() for name, v in arrays.items()]
    counts = nc.dram_tensor("counts_dram", (relations, -(-n // 128), 128, 128 * -(-n // 128)), mybir.dt.int16, kind="Internal").ap()
    out = nc.dram_tensor("out", (n, d), mybir.dt.float32, kind="ExternalOutput").ap()
    gat_rgcn_kernel(nc, *args, counts, out)
    return run_bass_kernel_spmd(nc, [arrays], core_ids=[0]).results[0]["out"]
```

```python
import concourse.bass as bass
from concourse import mybir
from contextlib import ExitStack


def gat_rgcn_kernel(nc, dst_cols, src_cols, type_cols, dst_units, xT, x, weights, a, bias, b_gate, counts_dram, out):
    f32 = mybir.dt.float32
    f32r = mybir.dt.float32r
    bf16 = mybir.dt.bfloat16
    f16 = mybir.dt.float16
    i32 = mybir.dt.int32
    i16 = mybir.dt.int16
    ALU = mybir.AluOpType
    ACT = mybir.ActivationFunctionType
    X = mybir.AxisListType.X
    ds = bass.ds

    N, D = x.shape
    P = 128
    KT = D // P
    NT = -(-N // P)
    NP = NT * P
    H2 = D // 2
    R = counts_dram.shape[0]
    EPS = 1e-5
    SLOPE = 0.1
    FLT_MAX = 3.4028234e38

    TILES = dst_cols.shape[1]
    PAIR = 2
    UNITS = dst_units.shape[0]
    WIN = P // R
    WINDOWS = NP // WIN
    HALF_W = WINDOWS // 2
    SUM_W = 5
    SPLIT = 320
    NE = N + N % 2
    NCOL = [(0, SPLIT), (SPLIT, NE - SPLIT)]

    RING = 4
    STEPS = R + 1
    ITEMS = 2 + 2 * KT
    GB = 3
    MEANS = 2 * KT

    def rows(t):
        return P if t < NT - 1 else N - P * (NT - 1)

    ctx = ExitStack()
    with ctx:
        def sem(name):
            return ctx.enter_context(nc.semaphore(name))

        def sb(name, shape, dt, where=ctx):
            return where.enter_context(nc.sbuf_tensor(name, shape, dt))

        M_hi = [sb("M_hi0", [P, KT, NP], f32r)]
        M_lo = [sb("M_lo0", [P, KT, NP], f32r)]
        w_raw = [sb(f"w_raw{b}", [P, H2], f32) for b in range(RING)]
        w_hi = [sb(f"w_hi{b}", [P, H2], f32r) for b in range(RING)]
        w_lo = [sb(f"w_lo{b}", [P, H2], f32r) for b in range(RING)]
        ident = sb("ident", [P, P], f32)
        ones = sb("ones", [P, P], f32)
        ones_r = sb("ones_r", [P, P], f32r)
        eps_col = sb("eps_col", [P, 1], f32)
        alr = sb("alr", [P, 2 * NT], f32)
        rowsum = sb("rowsum", [P, NT], f32)
        mv = sb("mv", [P, NT, 2], f32)
        rstd = sb("rstd", [P, NT], f32)
        stats = sb("stats", [P, 2, 2, 6], f32)

        with ExitStack() as counting:
            sb("under_M_lo1", [P, KT, NP], f32, counting)
            ints = sb("ints", [P, 3, TILES], i32, counting)
            src_f = sb("src_f", [P, TILES], f32, counting)
            q_f = sb("q_f", [P, TILES], f32, counting)
            type_f = sb("type_f", [P, TILES], f32, counting)
            units_i = sb("units_i", [UNITS, PAIR * P], i32, counting)
            unit_mm = sb("unit_mm", [UNITS, 2], f32, counting)
            unit_diag = sb("unit_diag", [UNITS, 2, UNITS + 1], f32, counting)
            iota_up = sb("iota_up", [P, UNITS], f32, counting)
            iota_down = sb("iota_down", [P, UNITS], f32, counting)
            reach = sb("reach", [WINDOWS, 2, UNITS], f32, counting)
            lohi = sb("lohi", [WINDOWS, 4], f32, counting)
            lohi_row = sb("lohi_row", [1, 2 * WINDOWS], i32, counting)
            win_edge = sb("win_edge", [P, 2], f32, counting)
            part_col = sb("part_col", [P, 1], f32, counting)
            win_base = sb("win_base", [P, WINDOWS], f32, counting)
            iota_node = sb("iota_node", [P, NP], f16, counting)
            zeros = sb("zeros", [P, P], bf16, counting)
            iota_i = sb("iota_i", [P, NP], i32, counting)
            hot_src = [sb(f"hot_src{s}", [P, NP], bf16, counting) for s in range(PAIR)]
            hot_q = [sb(f"hot_q{s}", [P, P], bf16, counting) for s in range(PAIR)]
            win_sb = [sb(f"win_sb{b}", [P, NP], f32, counting) for b in range(2)]
        M1 = sb("M1", [P, 2, KT, NP], f32r)
        M_lo.append(M1[:, 0, :, :])
        M_hi.append(M1[:, 1, :, :])
        h_parts = M1[:, :, :, :].rearrange("p s a b -> p s (a b)").rearrange("p s (l t n) -> p (s l) t n", l=2, t=NT)

        def h_part(low, half, t, p=P):
            return h_parts[0:p, ds(2 * half + low, 1), t, :].rearrange("p o n -> p (o n)")

        with ExitStack() as early:
            counts = sb("counts", [P, NT, R, NP], i16, early)
            counts_all = sb("counts_all", [P, NT, NP], f32, early)
            count_f = sb("count_f", [P, NT, SUM_W * WIN], f32, early)
            count_sum = sb("count_sum", [P, NT, SUM_W * WIN], f32, early)
            junk = sb("junk", [P, 2, H2], f32, early)
            dots = sb("dots", [P, 4 * NT], f32, early)
            diag = sb("diag", [P, NT, P], f32, early)
            a_bc = sb("a_bc", [P, 2 * D], f32, early)
            with ExitStack() as first:
                xT_raw = sb("xT_raw", [P, KT, N], f32, first)
            att = sb("att", [P, NT, NP], f32, early)

        with ExitStack() as late:
            x1_hi = sb("x1_hi", [P, NT, D], f32r, late)
            x1_lo = sb("x1_lo", [P, NT, D], f32r, late)
            u = sb("u", [P, NT, D], f32, late)
            bias_bc = sb("bias_bc", [P, D], f32, late)
            bg_bc = sb("bg_bc", [P, D], f32, late)
            with ExitStack() as elu:
                gt = [sb(f"gt{b}", [P, D], f32, elu) for b in range(2)]
                et = [sb(f"et{b}", [P, D], f32, elu) for b in range(2)]
            with ExitStack() as agg:
                C_hi = sb("C_hi", [P, NT, NP], f32r, agg)
                inv = sb("inv", [P, NE], f32, agg)
                mt = [sb(f"mt{b}", [P, SPLIT], f32, agg) for b in range(4)]
                c16 = sb("c16", [P, NT, NP], i16, agg)
            with ExitStack() as final:
                xf = sb("xf", [P, NT, D], f32, final)
                zt = [sb(f"zt{b}", [P, H2], f32, final) for b in range(2)]

        ps = ctx.enter_context(nc.psum_tensor("ps", [P, 8 * H2], f32))

        def bank(b, p=P, c0=0, c=H2):
            return ps[0:p, b * H2 + c0:b * H2 + c0 + c]

        def pair(b, p=P):
            return ps[0:p, 2 * b * H2:2 * (b + 1) * H2]

        edges_here = sem("edges_here")
        xT_here = [sem(f"xT_here{k}") for k in range(KT)]
        a_here = sem("a_here")
        bias_here = sem("bias_here")
        x_here = sem("x_here")
        raw_here = [sem(f"raw_here{b}") for b in range(RING)]
        w_hi_done = sem("w_hi_done")
        w_lo_done = sem("w_lo_done")
        w_used = sem("w_used")
        pool_consts = sem("pool_consts")
        pool_step = sem("pool_step")
        dve_step = sem("dve_step")
        act_step = sem("act_step")
        consts_done = sem("consts_done")
        units_diag_done = sem("units_diag_done")
        units_bcast = sem("units_bcast")
        lohi_done = sem("lohi_done")
        lohi_turned = sem("lohi_turned")
        row_done = sem("row_done")
        built = [sem(f"built{s}") for s in range(PAIR)]
        slot_free = [sem(f"slot_free{s}") for s in range(PAIR)]
        window_counted = sem("window_counted")
        window_copied = sem("window_copied")
        turned = sem("turned")
        turned_read = sem("turned_read")
        flushed = sem("flushed")
        summed = sem("summed")
        xT_hi_done = sem("xT_hi_done")
        xT_lo_done = sem("xT_lo_done")
        u_ready = sem("u_ready")
        u_drained = sem("u_drained")
        h_hi_done = sem("h_hi_done")
        diag_done = sem("diag_done")
        ar_bcast = sem("ar_bcast")
        sum_done = sem("sum_done")
        leaky_done = sem("leaky_done")
        exp_done = sem("exp_done")
        att_done = sem("att_done")
        attT_ready = sem("attT_ready")
        attT_hi_done = sem("attT_hi_done")
        attT_lo_done = sem("attT_lo_done")
        hp_ready = sem("hp_ready")
        elu_in = sem("elu_in")
        hp_read = sem("hp_read")
        elu_exp = sem("elu_exp")
        y_done = sem("y_done")
        std_done = sem("std_done")
        x1_done = sem("x1_done")
        x1_hi_done = sem("x1_hi_done")
        x1_lo_done = sem("x1_lo_done")
        x1T_ready = sem("x1T_ready")
        x1T_hi_done = sem("x1T_hi_done")
        x1T_lo_done = sem("x1T_lo_done")
        u_init = sem("u_init")
        c16_here = sem("c16_here")
        C_ready = sem("C_ready")
        g_ready = sem("g_ready")
        g_drained = sem("g_drained")
        inv_ready = sem("inv_ready")
        m_hi_done = sem("m_hi_done")
        m_lo_done = sem("m_lo_done")
        xt2_ready = sem("xt2_ready")
        xt2_hi_done = sem("xt2_hi_done")
        xt2_lo_done = sem("xt2_lo_done")
        uT_ready = sem("uT_ready")
        uT_hi_done = sem("uT_hi_done")
        uT_lo_done = sem("uT_lo_done")
        tanh_done = sem("tanh_done")
        xf_done = sem("xf_done")
        d_done = sem("d_done")
        var_done = sem("var_done")
        std2_done = sem("std2_done")
        y2_done = sem("y2_done")
        out_done = sem("out_done")

        SEG_W = 0
        SEG_U = 2
        SEG_G = SEG_U + 2 * STEPS
        SEGS = SEG_G + 4
        BANKS_G = NT * (SEG_G)

        def chunk_rows(n, k):
            if n < SEG_G:
                return (n // 2) * D + k * P, (n % 2) * H2
            m = n - SEG_G
            return (STEPS + 1 + (1 - m % 2)) * D + k * P, (m // 2) * H2

        def closes(n):
            return not isinstance(n, int) or n < SEG_G or n % 2 == 1

        def used_before(n):
            if not isinstance(n, int) or n < SEG_G:
                return n * (KT - 1)
            return SEG_G * (KT - 1) + (n - SEG_G) * KT - (n - SEG_G) // 2

        def filled(n):
            if not isinstance(n, int) or n < SEG_G:
                return n * NT + NT
            return BANKS_G + NT * ((n - SEG_G) // 2 + 1)

        def items(v):
            return [divmod(i, NT) for i in range(v * KT * NT // HALF_W, (v + 1) * KT * NT // HALF_W)]

        def chunk_ends(v):
            return [k for k, t in items(v) if t == NT - 1]

        block = ctx.enter_context(nc.Block())

        @block.sync
        def _(sp):
            def load_chunk(n, k, at=None, first=False):
                if not first:
                    sp.wait_ge(w_lo_done, 8 * n + k - RING + 1)
                r0, c0 = at or chunk_rows(n, k)
                sp.dma_start(w_raw[k % RING][:, :], weights[ds(r0, P), c0:c0 + H2]).then_inc(raw_here[k % RING], 16)

            def load_ahead(n, last=False):
                for k in range(KT):
                    if k < KT - RING:
                        load_chunk(n, k + RING)
                    elif not last:
                        load_chunk(n + 1, k + RING - KT)

            sp.dma_start(ints[:, 0, :], dst_cols).then_inc(edges_here, 16)
            sp.dma_start(ints[:, 1, :], src_cols).then_inc(edges_here, 16)
            sp.dma_start(ints[:, 2, :], type_cols).then_inc(edges_here, 16)
            sp.dma_start(units_i[:, :], dst_units).then_inc(edges_here, 16)
            for k in range(KT):
                if k < RING:
                    load_chunk(0, k, first=True)
                sp.dma_start(xT_raw[:, k, :], xT[k * P:(k + 1) * P, :]).then_inc(xT_here[k], 16)
            sp.dma_start(a_bc[:, :], a[0, :].partition_broadcast(P)).then_inc(a_here, 16)
            load_ahead(0)
            load_ahead(1)
            sp.wait_ge(turned_read, 2 * WINDOWS + 1)
            for m in range(NT):
                sp.dma_start(counts_dram[:, m, :, :].rearrange("r p n -> p r n"), counts[:, m, :, :]).then_inc(flushed, 16)
            sp.wait_ge(attT_lo_done, NT)
            sp.wait_ge(flushed, 16 * NT)
            sp.dma_start(u[:, 0:NT - 1, :], x[0:P * (NT - 1), :].rearrange("(t p) d -> p t d", p=P)).then_inc(x_here, 16)
            sp.dma_start(u[0:rows(NT - 1), NT - 1, :], x[P * (NT - 1):N, :]).then_inc(x_here, 16)
            sp.dma_start(bias_bc[:, :], bias.partition_broadcast(P)).then_inc(bias_here, 16)
            sp.dma_start(bg_bc[:, :], b_gate.partition_broadcast(P)).then_inc(bias_here, 16)
            sp.dma_start(c16[:, :, :], counts_dram[0, :, :, :].rearrange("m p n -> p m n")).then_inc(c16_here, 16)

            def step_loads(i, last):
                for h in range(2):
                    n = 2 * i + SEG_U + h
                    for k in range(KT - RING):
                        load_chunk(n, k + RING, at=((i + 1) * D + (k + RING) * P, h * H2))
                    for k in range(RING):
                        load_chunk(n + 1, k, at=((i + 1 + h) * D + k * P, (1 - h) * H2))
                if not last:
                    sp.wait_ge(C_ready, i + 1)
                    sp.dma_start(c16[:, :, :], counts_dram[ds(i + 1, 1), :, :, :].rearrange("o m p n -> p (o m) n"))\
                      .then_inc(c16_here, 16)

            with sp.Fori(0, R // 2 - 1) as j:
                for s in range(2):
                    step_loads(2 * j + s, False)
            step_loads(R - 2, False)
            step_loads(R - 1, True)
            for n in range(SEG_U + 2 * R, SEGS):
                load_ahead(n, last=n == SEGS - 1)
            for t in range(NT):
                sp.wait_ge(y2_done, t + 1)
                sp.dma_start(out[t * P:t * P + rows(t), :], u[0:rows(t), t, :]).then_inc(out_done, 16)
            sp.wait_ge(out_done, 16 * NT)

        @block.gpsimd
        def _(pool):
            steps = [0]

            def step(ins):
                steps[0] += 1
                ins.then_inc(pool_step, 1)
                pool.wait_ge(pool_step, steps[0])

            pool.sem_inc(m_lo_done, 4)
            pool.iota(iota_i[:, :], pattern=[[1, NP]], base=0, channel_multiplier=0).then_inc(pool_consts, 1)
            pool.iota(part_col[:, :], pattern=[[0, 1]], base=0, channel_multiplier=1,
                      allow_small_or_imprecise_dtypes=True).then_inc(pool_consts, 1)
            pool.iota(iota_up[:, :], pattern=[[1, UNITS]], base=1, channel_multiplier=0,
                      allow_small_or_imprecise_dtypes=True).then_inc(pool_consts, 1)
            pool.iota(iota_down[:, :], pattern=[[-1, UNITS]], base=1000, channel_multiplier=0,
                      allow_small_or_imprecise_dtypes=True).then_inc(pool_consts, 1)
            pool.iota(win_base[:, :], pattern=[[P, WINDOWS]], base=0, channel_multiplier=0,
                      allow_small_or_imprecise_dtypes=True).then_inc(pool_consts, 1)

            def split_chunk(n, k):
                pool.wait_ge(w_hi_done, 8 * n + k + 1)
                pool.tensor_tensor(w_lo[k % RING][:, :], w_raw[k % RING][:, :], w_hi[k % RING][:, :].bitcast(f32),
                                   ALU.subtract).then_inc(w_lo_done, 1)

            def split_ahead(n, last=False):
                for k in range(KT):
                    if k < KT - RING:
                        split_chunk(n, k + RING)
                    elif not last:
                        split_chunk(n + 1, k + RING - KT)

            def add_relations(half, v):
                pool.wait_ge(turned_read, 2 * (HALF_W * half + v + 1) + 1)
                cols = ds((HALF_W * half + v + 1 - SUM_W) * WIN, SUM_W * WIN)
                n = [(v + 1) // SUM_W * 2 * R - 2 * R]

                def ordered(ins):
                    n[0] += 1
                    ins.then_inc(summed, 1)
                    pool.wait_ge(summed, (HALF_W // SUM_W * 2 * R) * half + n[0])

                ordered(pool.tensor_copy(count_sum[:, :, :], counts[:, :, 0, cols]))
                for r in range(1, R):
                    ordered(pool.tensor_copy(count_f[:, :, :], counts[:, :, r, cols]))
                    ordered(pool.tensor_tensor(count_sum[:, :, :], count_sum[:, :, :], count_f[:, :, :], ALU.add))
                ordered(pool.tensor_copy(counts_all[:, :, cols], count_sum[:, :, :]))

            for k in range(KT):
                if k < RING:
                    split_chunk(0, k)
                pool.wait_ge(xT_hi_done, k + 1)
                pool.tensor_tensor(M_lo[0][:, k, 0:N], xT_raw[:, k, :], M_hi[0][:, k, 0:N].bitcast(f32),
                                   ALU.subtract).then_inc(xT_lo_done, 1)
            with pool.Fori(0, 2) as half:
                for v in range(HALF_W):
                    for k in chunk_ends(v):
                        split_chunk(half + (k + RING) // KT, (k + RING) % KT)
                    if v % SUM_W == SUM_W - 1:
                        add_relations(half, v)
            for t in range(NT):
                pool.wait_ge(x1_hi_done, t + 1)
                pool.tensor_tensor(x1_lo[0:rows(t), t, :], u[0:rows(t), t, :], x1_hi[0:rows(t), t, :].bitcast(f32),
                                   ALU.subtract).then_inc(x1_lo_done, 1)

            def means(i, odd, half):
                for e in range(half * MEANS // 2, (half + 1) * MEANS // 2):
                    c0, cn = NCOL[e % 2]
                    pool.wait_ge(m_hi_done, MEANS * i + e + 1)
                    pool.tensor_tensor(M_lo[1 - odd][:, e // 2, c0:c0 + cn], mt[e % 4][:, 0:cn],
                                       M_hi[1 - odd][:, e // 2, c0:c0 + cn].bitcast(f32), ALU.subtract)\
                        .then_inc(m_lo_done, 1)

            def step_work(i, odd):
                for half in range(2):
                    split_ahead(2 * i + SEG_U + half)
                    means(i, odd, half)

            with pool.Fori(0, R // 2) as j:
                for s in range(2):
                    step_work(2 * j + s, s)
            split_ahead(SEG_U + 2 * R)
            split_ahead(SEG_U + 2 * R + 1)
            split_ahead(SEG_G)
            for t in range(NT):
                r = slice(0, rows(t))
                if t == 0:
                    pool.wait_ge(g_drained, 3 + ITEMS * R)
                pool.tensor_tensor(xf[r, t, :], x1_hi[r, t, :].bitcast(f32), x1_lo[r, t, :].bitcast(f32), ALU.add)\
                    .then_inc(xf_done, 1)
            split_ahead(SEG_G + 1)
            for t in range(NT):
                r = slice(0, rows(t))
                pool.wait_ge(tanh_done, t + 1)
                pool.wait_ge(xf_done, t + 1)
                pool.tensor_tensor(u[r, t, :], u[r, t, :], xf[r, t, :], ALU.subtract).then_inc(d_done, 1)
            split_ahead(SEG_G + 2)
            split_ahead(SEG_G + 3, last=True)

        @block.scalar
        def _(act):
            act.sem_inc(window_copied, 1)
            act.sem_inc(turned_read, 1)

            def split_chunk(n, k, first=False):
                act.wait_ge(raw_here[k % RING], 32 * n + 16 * (k // RING) + 16)
                if not first:
                    m, j = (n, k - RING) if k >= RING else (n - 1, k + KT - RING)
                    if closes(m) and j == KT - 1:
                        act.wait_ge(u_ready, filled(m))
                    else:
                        act.wait_ge(w_used, used_before(m) + j + 1)
                nc.scalar.copy(w_hi[k % RING][:, :], w_raw[k % RING][:, :]).then_inc(w_hi_done, 1)

            def split_ahead(n, last=False):
                for k in range(KT):
                    if k < KT - RING:
                        split_chunk(n, k + RING)
                    elif not last:
                        split_chunk(n + 1, k + RING - KT)

            for k in range(KT):
                if k < RING:
                    split_chunk(0, k, first=True)
                act.wait_ge(xT_here[k], 16)
                nc.scalar.copy(M_hi[0][:, k, 0:N], xT_raw[:, k, :]).then_inc(xT_hi_done, 1)

            def place(w, part):
                blocks = [(0, NT - 1), (NT - 1, NT)][part]
                act.wait_ge(turned, 2 * w + part + 1)
                nc.scalar.copy(counts[:, blocks[0]:blocks[1], :, ds(WIN * w, WIN)],
                               bank(7, c=(blocks[1] - blocks[0]) * P).rearrange("p (m d r) -> p m r d", d=WIN, r=R))\
                  .then_inc(turned_read, 1)

            with act.Fori(0, 2) as half:
                for v in range(HALF_W):
                    w = HALF_W * half + v
                    act.wait_ge(window_counted, w + 1)
                    nc.scalar.copy(win_sb[v % 2][:, :].rearrange("p (b n) -> p b n", b=2),
                                   ps[:, 5 * H2:7 * H2].rearrange("p (b n) -> p b n", b=2)[:, :, 0:SPLIT])\
                      .then_inc(window_copied, 1)
                    if v:
                        place(w - 1, 1)
                    place(w, 0)
                    if v == HALF_W - 1:
                        place(w, 1)
                    for k in chunk_ends(v):
                        split_chunk(half + (k + RING) // KT, (k + RING) % KT)
                for t in range(NT):
                    act.wait_ge(u_ready, NT * half + t + 1)
                    nc.scalar.copy(h_part(0, half, t, rows(t)), bank(t, rows(t))).then_inc(h_hi_done, 1)
            act.wait_ge(ar_bcast, 1)
            act.wait_ge(diag_done, 1)
            for t in range(NT):
                nc.scalar.activation(att[0:rows(t), t, :].rearrange("p (b n) -> p b n", b=2),
                                     ps[0:rows(t), 5 * H2:7 * H2].rearrange("p (b n) -> p b n", b=2)[:, :, 0:SPLIT],
                                     ACT.Identity, bias=alr[0:rows(t), t:t + 1]).then_inc(sum_done, 1)
            for t in range(NT):
                act.wait_ge(leaky_done, t + 1)
                nc.scalar.activation(att[0:rows(t), t, :], att[0:rows(t), t, :], ACT.Exp, scale=-1.0).then_inc(exp_done, 1)
            for t in range(NT):
                act.wait_ge(attT_ready, t + 1)
                nc.scalar.copy(M_hi[0][0:rows(t), t, 0:N], pair(t % 3, rows(t))[:, 0:N]).then_inc(attT_hi_done, 1)
            for t in range(NT):
                act.wait_ge(elu_in, t + 1)
                nc.scalar.activation(et[t % 2][0:rows(t), :], et[t % 2][0:rows(t), :], ACT.Exp).then_inc(elu_exp, 1)
            act.wait_ge(y_done, NT)
            nc.scalar.activation(rstd[:, :], mv[:, :, 1], ACT.Sqrt, bias=eps_col[:, :]).then_inc(std_done, 1)
            for t in range(NT):
                act.wait_ge(x1_done, t + 1)
                nc.scalar.copy(x1_hi[0:rows(t), t, :], u[0:rows(t), t, :]).then_inc(x1_hi_done, 1)
                act.wait_ge(x1T_ready, t + 1)
                nc.scalar.copy(M_hi[0][:, :, t * P:t * P + rows(t)],
                               pair(t % 3).rearrange("p (k n) -> p k n", k=KT)[:, :, 0:rows(t)]).then_inc(x1T_hi_done, 1)

            def means(i, odd, half):
                for e in range(half * MEANS // 2, (half + 1) * MEANS // 2):
                    c0, cn = NCOL[e % 2]
                    act.wait_ge(g_drained, ITEMS * i + e + 2 + 3 + 1)
                    nc.scalar.copy(M_hi[1 - odd][:, e // 2, c0:c0 + cn], mt[e % 4][:, 0:cn]).then_inc(m_hi_done, 1)

            def step_work(i, odd):
                for half in range(2):
                    split_ahead(2 * i + SEG_U + half)
                    means(i, odd, half)

            with act.Fori(0, R // 2) as j:
                for s in range(2):
                    step_work(2 * j + s, s)

            for half in range(2):
                split_ahead(SEG_U + 2 * R + half)
                for t, kh in [(t, kh) for t in range(NT) for kh in range(2)][half * NT:(half + 1) * NT]:
                    act.wait_ge(xt2_ready, 2 * (2 * t + kh) + 1)
                    nc.scalar.copy(M_hi[1][:, 4 * kh:4 * kh + 4, t * P:t * P + rows(t)],
                                   bank(5 + 2 * (2 * t + kh) % GB).rearrange("p (k n) -> p k n", k=4)[:, :, 0:rows(t)])\
                      .then_inc(xt2_hi_done, 1)
            split_ahead(SEG_G)
            for t in range(NT):
                for kh in range(2):
                    it = 2 * t + kh
                    act.wait_ge(uT_ready, it + 1)
                    nc.scalar.copy(M_hi[0][:, 4 * kh:4 * kh + 4, t * P:t * P + rows(t)],
                                   bank(5 + it % GB).rearrange("p (k n) -> p k n", k=4)[:, :, 0:rows(t)])\
                      .then_inc(uT_hi_done, 1)
            split_ahead(SEG_G + 1)
            for t in range(NT):
                nc.scalar.activation(u[0:rows(t), t, :], u[0:rows(t), t, :], ACT.Tanh).then_inc(tanh_done, 1)
            split_ahead(SEG_G + 2)
            split_ahead(SEG_G + 3, last=True)
            for t in range(NT):
                act.wait_ge(var_done, t + 1)
                nc.scalar.activation(rstd[0:rows(t), t:t + 1], mv[0:rows(t), t, 1:2], ACT.Sqrt,
                                     bias=eps_col[0:rows(t), :]).then_inc(std2_done, 1)

        @block.vector
        def _(dve):
            steps = [0]

            def step(ins):
                steps[0] += 1
                ins.then_inc(dve_step, 1)
                dve.wait_ge(dve_step, steps[0])

            v = nc.vector
            dve.sem_inc(u_drained, NT)
            dve.sem_inc(g_drained, 3)
            v.memset(ones[:, :], 1.0)
            v.memset(zeros[:, :], 0.0)
            v.memset(ones_r[:, :].bitcast(f32), 1.0)
            v.memset(eps_col[:, :], EPS)
            v.memset(rowsum[:, :], 1.0)
            v.memset(mv[:, :, :], 1.0)
            step(v.memset(dots[:, :], 0.0))
            dve.wait_ge(pool_consts, 5)
            step(v.tensor_copy(iota_node[:, :], iota_i[:, :]))
            step(v.tensor_scalar(ident[:, :], iota_node[:, 0:P], part_col[:, :], None, ALU.is_equal))
            v.tensor_scalar(win_edge[:, 0:1], part_col[:, :], float(WIN), None, ALU.mult)
            step(v.tensor_scalar(win_edge[:, 1:2], part_col[:, :], float(WIN), float(WIN - 1), ALU.mult, ALU.add))
            dve.wait_ge(edges_here, 64)
            v.tensor_reduce(unit_mm[:, 0:1], units_i[:, :], X, ALU.max)
            step(v.tensor_reduce(unit_mm[:, 1:2], units_i[:, :], X, ALU.min))
            for c in range(2):
                d = v.tensor_scalar(unit_diag[:, c, 0:UNITS], ident[0:UNITS, 0:UNITS], unit_mm[:, c:c + 1], None, ALU.mult)
            d.then_inc(units_diag_done, 1)
            v.tensor_copy(src_f[:, :], ints[:, 1, :])
            step(v.tensor_copy(q_f[:, :], ints[:, 0, :]))
            step(v.tensor_copy(type_f[:, :], ints[:, 2, :]))
            step(v.scalar_tensor_tensor(q_f[:, :], q_f[:, :], float(R), type_f[:, :], ALU.mult, ALU.add))
            dve.wait_ge(units_bcast, 1)
            step(v.scalar_tensor_tensor(reach[:, 0, :], ps[0:WINDOWS, 4 * H2:4 * H2 + UNITS], win_edge[0:WINDOWS, 0:1],
                                        iota_down[0:WINDOWS, :], ALU.is_ge, ALU.mult))
            step(v.scalar_tensor_tensor(reach[:, 1, :], ps[0:WINDOWS, 5 * H2:5 * H2 + UNITS], win_edge[0:WINDOWS, 1:2],
                                        iota_up[0:WINDOWS, :], ALU.is_le, ALU.mult))
            step(v.tensor_reduce(lohi[:, 0:2], reach[:, :, :], X, ALU.max))
            step(v.tensor_scalar(lohi[:, 2:3], lohi[:, 0:1], -1.0, 1000.0, ALU.mult, ALU.add))
            v.tensor_scalar(lohi[:, 3:4], lohi[:, 2:3], 1.0, lohi[:, 1:2], ALU.add, ALU.max).then_inc(lohi_done, 1)
            dve.wait_ge(lohi_turned, 1)
            v.tensor_copy(lohi_row[:, 0:WINDOWS], ps[0:1, 6 * H2:6 * H2 + WINDOWS])
            v.tensor_copy(lohi_row[:, WINDOWS:2 * WINDOWS], ps[0:1, 7 * H2:7 * H2 + WINDOWS]).then_inc(row_done, 1)
            dve.wait_ge(row_done, 1)

            turn = dve.alloc_register("dve_turn")
            dve.reg_mov(turn, 0)
            with dve.Fori(0, 2) as half:
                for v_ in range(HALF_W):
                    w = HALF_W * half + v_
                    lo = dve.value_load(lohi_row[0:1, ds(w, 1)], min_val=0, max_val=UNITS - 1)
                    hi = dve.value_load(lohi_row[0:1, ds(w + WINDOWS, 1)], min_val=1, max_val=UNITS)
                    with dve.Fori(lo, hi) as unit:
                        dve.reg_add(turn, turn, 1)
                        n = dve.snap(turn, min_val=1, max_val=WINDOWS * UNITS)
                        for s in range(PAIR):
                            col = ds(unit * PAIR + s, 1)
                            dve.wait_ge(slot_free[s], n)
                            v.tensor_scalar(hot_src[s][:, :], iota_node[:, :], src_f[:, col], None, ALU.is_equal)
                            v.tensor_scalar(hot_q[s][:, :], iota_node[:, 0:P], win_base[:, ds(w, 1)], q_f[:, col],
                                            ALU.add, ALU.is_equal).then_inc(built[s], 1)
                for t in range(NT):
                    r = slice(0, rows(t))
                    dve.wait_ge(h_hi_done, NT * half + t + 1)
                    if t == 0:
                        dve.wait_ge(a_here, 16)
                    for lr in range(2):
                        v.scalar_tensor_tensor(junk[r, lr, :], bank(t, rows(t)), 1.0, a_bc[r, ds(half * H2 + lr * D, H2)],
                                               ALU.mult, ALU.mult, accum_out=dots[r, ds(half * 2 * NT + lr * NT + t, 1)])
                    v.tensor_tensor(h_part(1, half, t, rows(t)), bank(t, rows(t)), h_part(0, half, t, rows(t)).bitcast(f32),
                                    ALU.subtract).then_inc(u_drained, 1)
                    dve.wait_ge(u_drained, NT * half + t + 1 + NT)
            step(v.tensor_tensor(alr[:, :], dots[:, 0:2 * NT], dots[:, 2 * NT:4 * NT], ALU.add))
            for t in range(NT):
                d = v.tensor_scalar(diag[:, t, :], ident[:, :], alr[:, NT + t:NT + t + 1], None, ALU.mult)
            d.then_inc(diag_done, 1)
            for t in range(NT):
                r = slice(0, rows(t))
                dve.wait_ge(sum_done, t + 1)
                v.scalar_tensor_tensor(att[r, t, :], att[r, t, :], SLOPE, att[r, t, :], ALU.mult, ALU.max)\
                    .then_inc(leaky_done, 1)
            dve.wait_ge(summed, 2 * HALF_W // SUM_W * 2 * R)
            for t in range(NT):
                r = slice(0, rows(t))
                dve.wait_ge(exp_done, t + 1)
                v.scalar_tensor_tensor(att[r, t, :], att[r, t, :], FLT_MAX, counts_all[r, t, :], ALU.min, ALU.mult,
                                       accum_out=rowsum[r, t:t + 1]).then_inc(att_done, 1)
            dve.wait_ge(att_done, NT)
            step(v.tensor_scalar(rowsum[:, :], rowsum[:, :], EPS, None, ALU.add))
            step(v.reciprocal(rowsum[:, :], rowsum[:, :]))
            for t in range(NT):
                r = slice(0, rows(t))
                dve.wait_ge(attT_hi_done, t + 1)
                v.tensor_tensor(M_lo[0][r, t, 0:N], pair(t % 3, rows(t))[:, 0:N], M_hi[0][r, t, 0:N].bitcast(f32),
                                ALU.subtract).then_inc(attT_lo_done, 1)
            dve.wait_ge(x_here, 32)

            def elu_start(t):
                r = slice(0, rows(t))
                dve.wait_ge(hp_ready, t + 1)
                v.tensor_scalar(et[t % 2][r, :], pair(t % 3, rows(t)), rowsum[r, t:t + 1], 0.0, ALU.mult, ALU.min)\
                    .then_inc(elu_in, 1)
                v.tensor_scalar(gt[t % 2][r, :], pair(t % 3, rows(t)), rowsum[r, t:t + 1], 0.0, ALU.mult, ALU.max)\
                    .then_inc(hp_read, 1)

            def elu_end(t):
                r = slice(0, rows(t))
                dve.wait_ge(elu_exp, t + 1)
                dve.wait_ge(hp_read, t + 1)
                step(v.scalar_tensor_tensor(gt[t % 2][r, :], et[t % 2][r, :], -1.0, gt[t % 2][r, :], ALU.add, ALU.add))
                step(v.tensor_tensor(u[r, t, :], gt[t % 2][r, :], u[r, t, :], ALU.add))
                for c in range(2):
                    s_ = v.bn_stats(stats[r, t % 2, c, :], u[r, t, c * H2:(c + 1) * H2])
                step(s_)
                v.bn_aggr(mv[r, t, :], stats[r, t % 2, :, :]).then_inc(y_done, 1)

            for t in range(NT):
                elu_start(t)
                if t:
                    elu_end(t - 1)
            elu_end(NT - 1)
            dve.wait_ge(std_done, 1)
            step(v.reciprocal(rstd[:, :], rstd[:, :]))
            for t in range(NT):
                r = slice(0, rows(t))
                v.tensor_scalar(u[r, t, :], u[r, t, :], mv[r, t, 0:1], rstd[r, t:t + 1], ALU.subtract, ALU.mult)\
                    .then_inc(x1_done, 1)
            for t in range(NT):
                dve.wait_ge(x1T_hi_done, t + 1)
                v.tensor_tensor(M_lo[0][:, :, t * P:t * P + rows(t)],
                                pair(t % 3).rearrange("p (k n) -> p k n", k=KT)[:, :, 0:rows(t)],
                                M_hi[0][:, :, t * P:t * P + rows(t)].bitcast(f32), ALU.subtract).then_inc(x1T_lo_done, 1)
            dve.wait_ge(x1_lo_done, NT)
            dve.wait_ge(bias_here, 32)
            for t in range(NT):
                d = v.tensor_copy(u[:, t, :], bias_bc[:, :])
            d.then_inc(u_init, 1)
            dve.wait_ge(u_init, 1)

            def convert_counts(i):
                dve.wait_ge(c16_here, 16 * i + 16)
                v.tensor_copy(C_hi[:, :, :], c16[:, :, :]).then_inc(C_ready, 1)

            def add_u(i, half, t):
                r = slice(0, rows(t))
                dve.wait_ge(u_ready, 2 * NT * i + NT * (SEG_U + half) + t + 1)
                v.tensor_tensor(u[r, t, half * H2:(half + 1) * H2], bank(t, rows(t)), u[r, t, half * H2:(half + 1) * H2],
                                ALU.add).then_inc(u_drained, 1)

            def invert(i, q):
                c0, cn = NCOL[q]
                dve.wait_ge(g_ready, ITEMS * i + q + 1)
                v.tensor_scalar(inv[:, c0:c0 + cn], bank(5 + q, c=cn), 1.0, None, ALU.max).then_inc(g_drained, 1)
                dve.wait_ge(g_drained, ITEMS * i + 3 + q + 1)
                v.reciprocal(inv[:, c0:c0 + cn], inv[:, c0:c0 + cn]).then_inc(inv_ready, 1)

            def scale_mean(i, e):
                q = e + 2
                c0, cn = NCOL[e % 2]
                if e == 0:
                    dve.wait_ge(inv_ready, 2 * i + 2)
                dve.wait_ge(g_ready, ITEMS * i + q + 1)
                dve.wait_ge(m_lo_done, MEANS * i + e + 1)
                v.tensor_tensor(mt[e % 4][:, 0:cn], bank(5 + q % GB, c=cn), inv[:, c0:c0 + cn], ALU.mult)\
                    .then_inc(g_drained, 1)

            def step_work(i):
                convert_counts(i)
                for half in range(2):
                    add_u(i, half, 0)
                    if half == 0:
                        invert(i, 0)
                        invert(i, 1)
                    for n in range(MEANS // 2):
                        scale_mean(i, half * MEANS // 2 + n)
                        if n < NT - 1:
                            add_u(i, half, n + 1)

            with dve.Fori(0, R // 2) as j:
                for s in range(2):
                    step_work(2 * j + s)

            for half in range(2):
                for t in range(NT):
                    add_u(R, half, t)
                for t, kh in [(t, kh) for t in range(NT) for kh in range(2)][half * NT:(half + 1) * NT]:
                    it = 2 * (2 * t + kh) + 1
                    dve.wait_ge(xt2_ready, it + 1)
                    v.tensor_copy(M_lo[1][:, 4 * kh:4 * kh + 4, t * P:t * P + rows(t)],
                                  bank(5 + it % GB).rearrange("p (k n) -> p k n", k=4)[:, :, 0:rows(t)])\
                        .then_inc(xt2_lo_done, 1)
            for t in range(NT):
                for kh in range(2):
                    it = 2 * t + kh
                    dve.wait_ge(uT_hi_done, it + 1)
                    v.tensor_tensor(M_lo[0][:, 4 * kh:4 * kh + 4, t * P:t * P + rows(t)],
                                    bank(5 + it % GB).rearrange("p (k n) -> p k n", k=4)[:, :, 0:rows(t)],
                                    M_hi[0][:, 4 * kh:4 * kh + 4, t * P:t * P + rows(t)].bitcast(f32), ALU.subtract)\
                        .then_inc(uT_lo_done, 1)
            for half in range(2):
                for t in range(NT):
                    r, c = slice(0, rows(t)), slice(half * H2, (half + 1) * H2)
                    z = zt[t % 2]
                    dve.wait_ge(u_ready, BANKS_G + NT * half + t + 1)
                    v.tensor_tensor(z[r, :], bank(t, rows(t)), bg_bc[r, c], ALU.add).then_inc(u_drained, 1)
                    dve.wait_ge(u_drained, BANKS_G + NT * half + t + 1 + NT)
                    dve.wait_ge(d_done, t + 1)
                    step(v.tensor_tensor(z[r, :], z[r, :], u[r, t, c], ALU.mult))
                    step(v.scalar_tensor_tensor(u[r, t, c], xf[r, t, c], 2.0, z[r, :], ALU.mult, ALU.add))
                    if half:
                        for hh in range(2):
                            s_ = v.bn_stats(stats[r, t % 2, hh, :], u[r, t, hh * H2:(hh + 1) * H2])
                        step(s_)
                        v.bn_aggr(mv[r, t, :], stats[r, t % 2, :, :]).then_inc(var_done, 1)
            for t in range(NT):
                r = slice(0, rows(t))
                dve.wait_ge(std2_done, t + 1)
                step(v.reciprocal(rstd[r, t:t + 1], rstd[r, t:t + 1]))
                v.tensor_scalar(u[r, t, :], u[r, t, :], mv[r, t, 0:1], rstd[r, t:t + 1], ALU.subtract, ALU.mult)\
                    .then_inc(y2_done, 1)

        @block.tensor
        def _(pe):
            mm = nc.tensor.matmul
            for s in range(PAIR):
                pe.sem_inc(slot_free[s], 1)

            pe.wait_ge(units_diag_done, 1)
            for c in range(2):
                last = mm(ps[0:WINDOWS, (4 + c) * H2:(4 + c) * H2 + UNITS], ones[0:UNITS, 0:WINDOWS],
                          unit_diag[:, c, 0:UNITS], start=True, stop=True)
            last.then_inc(units_bcast, 1)
            pe.wait_ge(lohi_done, 1)
            for c in range(2):
                last = mm(ps[0:1, (6 + c) * H2:(6 + c) * H2 + WINDOWS], lohi[:, 2 + c:3 + c],
                          ident[0:WINDOWS, 0:WINDOWS], start=True, stop=True)
            last.then_inc(lohi_turned, 1)

            pe.wait_ge(row_done, 1)
            turn = pe.alloc_register("pe_turn")
            pe.reg_mov(turn, 0)
            def product_item(k, t, lhs_hi, lhs_lo, opens, closes_):
                c = slice(t * P, t * P + rows(t))
                o = bank(t, rows(t))
                mm(o, lhs_hi[:, k, c], w_hi[k % RING][:, :], start=opens, stop=False)
                mm(o, lhs_lo[:, k, c], w_hi[k % RING][:, :], start=False, stop=False)
                last = mm(o, lhs_hi[:, k, c], w_lo[k % RING][:, :], start=False, stop=closes_)
                if closes_:
                    last.then_inc(u_ready, 1)
                elif t == NT - 1:
                    last.then_inc(w_used, 1)

            def turn_back(w, v, part):
                pe.wait_ge(turned_read, 2 * w + part + 1)
                if part == 0:
                    pe.wait_ge(window_copied, w + 2)
                for j, m in enumerate(range(NT - 1) if part == 0 else [NT - 1]):
                    last = nc.tensor.transpose(bank(7, c0=j * P, c=P), win_sb[v % 2][:, m * P:(m + 1) * P], ident[:, :])
                last.then_inc(turned, 1)

            with pe.Fori(0, 2) as half:
                for v in range(HALF_W):
                    w = HALF_W * half + v
                    lo = pe.value_load(lohi_row[0:1, ds(w, 1)], min_val=0, max_val=UNITS - 1)
                    hi = pe.value_load(lohi_row[0:1, ds(w + WINDOWS, 1)], min_val=1, max_val=UNITS)
                    pe.wait_ge(window_copied, w + 1)
                    for c in range(2):
                        mm(bank(5 + c, c=2), zeros[:, :], zeros[:, 0:2], start=True, stop=False, skip_group_check=True)
                    with pe.Fori(lo, hi) as unit:
                        pe.reg_add(turn, turn, 1)
                        n = pe.snap(turn, min_val=1, max_val=WINDOWS * UNITS)
                        for s in range(PAIR):
                            pe.wait_ge(built[s], n)
                            for c in range(2):
                                last = mm(bank(5 + c, c=SPLIT), hot_q[s][:, :], hot_src[s][:, c * SPLIT:(c + 1) * SPLIT],
                                          start=False, stop=False, skip_group_check=True)
                            last.then_inc(slot_free[s], 1)
                    for c in range(2):
                        last = mm(bank(5 + c, c=2), zeros[:, :], zeros[:, 0:2], start=False, stop=True,
                                  skip_group_check=True)
                    last.then_inc(window_counted, 1)
                    if v:
                        turn_back(w - 1, v - 1, 1)
                    for k, t in items(v):
                        if t == 0:
                            pe.wait_ge(w_lo_done, 8 * half + k + 1)
                            pe.wait_ge(xT_lo_done, k + 1)
                        if k == 0:
                            pe.wait_ge(u_drained, NT * half + t + 1)
                        product_item(k, t, M_hi[0], M_lo[0], k == 0, k == KT - 1)
                    turn_back(w, v, 0)
                    if v == HALF_W - 1:
                        turn_back(w, v, 1)

            def product(n, lhs_hi, lhs_lo, before, open_=True, close=True):
                for k in range(KT):
                    pe.wait_ge(w_lo_done, 8 * n + k + 1)
                    for t in range(NT):
                        if k == 0 and open_ and before is not None:
                            pe.wait_ge(u_drained, before + t + 1)
                        product_item(k, t, lhs_hi, lhs_lo, open_ and k == 0, close and k == KT - 1)

            pe.wait_ge(turned_read, 2 * WINDOWS + 1)
            pe.wait_ge(diag_done, 1)
            for c in range(2):
                last = mm(bank(5 + c, c=SPLIT), ones[:, :], diag[:, :, :].rearrange("p a b -> p (a b)")[:, c * SPLIT:(c + 1) * SPLIT],
                          start=True, stop=True)
            last.then_inc(ar_bcast, 1)
            pe.wait_ge(att_done, NT)
            for d in range(NT):
                if d >= 3:
                    pe.wait_ge(attT_lo_done, d - 2)
                for t in range(NT):
                    last = nc.tensor.transpose(pair(d % 3)[:, t * P:t * P + rows(t)], att[0:rows(t), t, d * P:(d + 1) * P],
                                               ident[0:rows(t), 0:rows(t)])
                last.then_inc(attT_ready, 1)
            pe.wait_ge(attT_lo_done, NT)
            for t in range(NT):
                if t >= 3:
                    pe.wait_ge(hp_read, t - 2)
                c = slice(t * P, t * P + rows(t))
                for half in range(2):
                    o = bank(2 * (t % 3) + half, rows(t))
                    for d in range(NT):
                        k = slice(0, rows(d))
                        mm(o, M_hi[0][k, d, c], h_parts[k, 2 * half, d, :], start=d == 0, stop=False)
                        mm(o, M_lo[0][k, d, c], h_parts[k, 2 * half, d, :], start=False, stop=False)
                        last = mm(o, M_hi[0][k, d, c], h_parts[k, 2 * half + 1, d, :], start=False, stop=d == NT - 1)
                last.then_inc(hp_ready, 1)
            for t in range(NT):
                pe.wait_ge(x1_done, t + 1)
                if t >= 3:
                    pe.wait_ge(x1T_lo_done, t - 2)
                for k in range(KT):
                    last = nc.tensor.transpose(pair(t % 3)[:, k * P:k * P + rows(t)], u[0:rows(t), t, k * P:(k + 1) * P],
                                               ident[0:rows(t), 0:rows(t)])
                last.then_inc(x1T_ready, 1)
            pe.wait_ge(x1T_lo_done, NT)

            def aggregate(i, half):
                if half == 0:
                    pe.wait_ge(C_ready, i + 1)
                for q in range(0 if half == 0 else 2 + MEANS // 2, 2 + (half + 1) * MEANS // 2):
                    c0, cn = NCOL[q % 2]
                    o = bank(5 + q % GB, c=cn)
                    pe.wait_ge(g_drained, ITEMS * i + q + 1)
                    for m in range(NT):
                        if q < 2:
                            last = mm(o, ones_r[:, :], C_hi[:, m, c0:c0 + cn], start=m == 0, stop=m == NT - 1)
                        else:
                            r, f = slice(0, rows(m)), slice((q - 2) // 2 * P, (q - 2) // 2 * P + P)
                            mm(o, x1_hi[r, m, f], C_hi[r, m, c0:c0 + cn], start=m == 0, stop=False)
                            last = mm(o, x1_lo[r, m, f], C_hi[r, m, c0:c0 + cn], start=False, stop=m == NT - 1)
                    last.then_inc(g_ready, 1)

            def step_work(i, odd):
                for half in range(2):
                    n = 2 * i + SEG_U + half
                    product(n, M_hi[odd], M_lo[odd], 2 * NT * i + NT * (SEG_U + half))
                    aggregate(i, half)
                pe.wait_ge(m_lo_done, MEANS * i + MEANS + 4)

            with pe.Fori(0, R // 2) as j:
                for s in range(2):
                    step_work(2 * j + s, s)
            for half in range(2):
                n = SEG_U + 2 * R + half
                product(n, M_hi[0], M_lo[0], NT * n)
                for t, kh in [(t, kh) for t in range(NT) for kh in range(2)][half * NT:(half + 1) * NT]:
                    for lo_, src in enumerate((x1_hi, x1_lo)):
                        it = 2 * (2 * t + kh) + lo_
                        if it >= GB:
                            b4 = it - GB
                            pe.wait_ge(xt2_lo_done if b4 % 2 else xt2_hi_done, b4 // 2 + 1)
                        elif it == 0:
                            pe.wait_ge(g_drained, ITEMS * R + 3)
                        for k in range(4):
                            f = slice((4 * kh + k) * P, (4 * kh + k + 1) * P)
                            last = nc.tensor.transpose(bank(5 + it % GB, c0=k * P, c=rows(t)),
                                                       src[0:rows(t), t, f].bitcast(f32), ident[0:rows(t), 0:rows(t)])
                        last.then_inc(xt2_ready, 1)
            pe.wait_ge(xt2_lo_done, 2 * NT)
            pe.wait_ge(xt2_hi_done, 2 * NT)
            product(SEG_G, M_hi[1], M_lo[1], BANKS_G, close=False)
            for t in range(NT):
                for kh in range(2):
                    it = 2 * t + kh
                    if it >= GB:
                        pe.wait_ge(uT_lo_done, it - GB + 1)
                    for k in range(4):
                        last = nc.tensor.transpose(bank(5 + it % GB, c0=k * P, c=rows(t)),
                                                   u[0:rows(t), t, (4 * kh + k) * P:(4 * kh + k + 1) * P],
                                                   ident[0:rows(t), 0:rows(t)])
                    last.then_inc(uT_ready, 1)
            pe.wait_ge(uT_lo_done, 2 * NT)
            product(SEG_G + 1, M_hi[0], M_lo[0], None, open_=False)
            product(SEG_G + 2, M_hi[1], M_lo[1], BANKS_G + NT, close=False)
            product(SEG_G + 3, M_hi[0], M_lo[0], None, open_=False)


def kernel(**inputs):
    import numpy as np
    import concourse.bacc as bacc
    from concourse import mybir
    from concourse.bass_utils import run_bass_kernel_spmd

    x = np.ascontiguousarray(inputs["x"])
    n, d = x.shape
    relations = inputs["L1_gnn_weight"].shape[0]
    edges = inputs["dst"].shape[0]
    tiles = 2 * -(-edges // 256)
    far = 1 << 20

    def padded(v, fill):
        row = np.full((tiles * 128,), fill, np.int32)
        row[:edges] = v
        return row

    dst = padded(inputs["dst"], far)
    w_gate = np.asarray(inputs["L1_gnn_w_gate"])
    arrays = {
        "dst_cols": np.ascontiguousarray(dst.reshape(tiles, 128).T),
        "src_cols": np.ascontiguousarray(padded(inputs["src"], 0).reshape(tiles, 128).T),
        "type_cols": np.ascontiguousarray(padded(inputs["edge_type_8"], 0).reshape(tiles, 128).T),
        "dst_units": dst.reshape(tiles // 2, 256),
        "xT": np.ascontiguousarray(x.T),
        "x": x,
        "weights": np.concatenate([np.asarray(inputs["L0_gnn_W"]), np.asarray(inputs["L1_gnn_root"]),
                                   np.asarray(inputs["L1_gnn_weight"]).reshape(relations * d, d), w_gate]),
        "a": np.ascontiguousarray(inputs["L0_gnn_a"]),
        "bias": np.ascontiguousarray(inputs["L1_gnn_bias"]),
        "b_gate": np.ascontiguousarray(inputs["L1_gnn_b_gate"]),
    }
    nc = bacc.Bacc("TRN2", target_bir_lowering=False, num_devices=1)
    args = [nc.dram_tensor(name, v.shape, mybir.dt.from_np(v.dtype), kind="ExternalInput").ap() for name, v in arrays.items()]
    counts = nc.dram_tensor("counts_dram", (relations, -(-n // 128), 128, 128 * -(-n // 128)), mybir.dt.int16, kind="Internal").ap()
    out = nc.dram_tensor("out", (n, d), mybir.dt.float32, kind="ExternalOutput").ap()
    gat_rgcn_kernel(nc, *args, counts, out)
    return run_bass_kernel_spmd(nc, [arrays], core_ids=[0]).results[0]["out"]
```

```python
import concourse.bass as bass
from concourse import mybir
from contextlib import ExitStack


def gat_rgcn_kernel(nc, dst_cols, src_cols, type_cols, dst_units, xT, x, weights, a, bias, b_gate, counts_dram, out):
    f32 = mybir.dt.float32
    f32r = mybir.dt.float32r
    bf16 = mybir.dt.bfloat16
    f16 = mybir.dt.float16
    i32 = mybir.dt.int32
    i16 = mybir.dt.int16
    ALU = mybir.AluOpType
    ACT = mybir.ActivationFunctionType
    X = mybir.AxisListType.X
    ds = bass.ds

    N, D = x.shape
    P = 128
    KT = D // P
    NT = -(-N // P)
    NP = NT * P
    H2 = D // 2
    R = counts_dram.shape[0]
    EPS = 1e-5
    SLOPE = 0.1
    FLT_MAX = 3.4028234e38

    TILES = dst_cols.shape[1]
    DEPTH = 2
    PAIR = 2
    HOT = PAIR * (NP + P)
    UNITS = dst_units.shape[0]
    WIN = P // R
    WINDOWS = NP // WIN
    HALF_W = WINDOWS // 2
    SUM_W = 5
    SPLIT = 320
    NE = N + N % 2
    NCOL = [(0, SPLIT), (SPLIT, NE - SPLIT)]

    RING = 4
    STEPS = R + 1
    ITEMS = 1 + 2 * KT
    GB = 3
    SUMS = 2 * KT

    def rows(t):
        return P if t < NT - 1 else N - P * (NT - 1)

    ctx = ExitStack()
    with ctx:
        def sem(name):
            return ctx.enter_context(nc.semaphore(name))

        def sb(name, shape, dt, where=ctx):
            return where.enter_context(nc.sbuf_tensor(name, shape, dt))

        M_hi = [sb("M_hi0", [P, KT, NP], f32r)]
        M_lo = [sb("M_lo0", [P, KT, NP], f32r)]
        w_raw = [sb(f"w_raw{b}", [P, H2], f32) for b in range(RING)]
        w_hi = [sb(f"w_hi{b}", [P, H2], f32r) for b in range(RING)]
        w_lo = [sb(f"w_lo{b}", [P, H2], f32r) for b in range(RING)]
        ident = sb("ident", [P, P], f32)
        ones = sb("ones", [P, P], f32)
        ones_r = sb("ones_r", [P, P], f32r)
        eps_col = sb("eps_col", [P, 1], f32)
        alr = sb("alr", [P, 2 * NT], f32)
        rowsum = sb("rowsum", [P, NT], f32)
        mv = sb("mv", [P, NT, 2], f32)
        scale = [sb(f"scale{b}", [P, NT], f32) for b in range(2)]
        rstd = sb("rstd", [P, NT], f32)
        stats = sb("stats", [P, 2, 2, 6], f32)

        with ExitStack() as counting:
            sb("under_M_lo1", [P, KT, NP], f32, counting)
            src_f = sb("src_f", [P, TILES], f32, counting)
            q_f = sb("q_f", [P, TILES], f32, counting)
            lohi_row = sb("lohi_row", [1, 2 * WINDOWS], i32, counting)
            iota_node = sb("iota_node", [P, NP], f16, counting)
            zeros = sb("zeros", [P, P], bf16, counting)
            hot = sb("hot", [P, DEPTH * HOT], bf16, counting)
            with ExitStack() as setup:
                ints = sb("ints", [P, 3, TILES], i32, setup)
                iota_i = sb("iota_i", [P, NP], i32, setup)
                part_col = sb("part_col", [P, 1], f32, setup)
                win_edge = sb("win_edge", [P, 2], f32, setup)
                lohi = sb("lohi", [WINDOWS, 4], f32, setup)
            win_sb = [sb(f"win_sb{b}", [P, NP], f32, counting) for b in range(2)]
        M1 = sb("M1", [P, 2, KT, NP], f32r)
        M_lo.append(M1[:, 0, :, :])
        M_hi.append(M1[:, 1, :, :])
        h_parts = M1[:, :, :, :].rearrange("p s a b -> p s (a b)").rearrange("p s (l t n) -> p (s l) t n", l=2, t=NT)

        def h_part(low, half, t, p=P):
            return h_parts[0:p, ds(2 * half + low, 1), t, :].rearrange("p o n -> p (o n)")

        with ExitStack() as early:
            counts = sb("counts", [P, NT, R, NP], i16, early)
            counts_all = sb("counts_all", [P, NT, NP], f32, early)
            count_f = sb("count_f", [P, NT, SUM_W * WIN], f32, early)
            count_sum = sb("count_sum", [P, NT, SUM_W * WIN], f32, early)
            with ExitStack() as setup:
                iota_q = sb("iota_q", [P, P], f32, setup)
                type_f = sb("type_f", [P, TILES], f32, setup)
                units_i = sb("units_i", [UNITS, PAIR * P], i32, setup)
                unit_mm = sb("unit_mm", [UNITS, 2], f32, setup)
                unit_diag = sb("unit_diag", [UNITS, 2, UNITS + 1], f32, setup)
                iota_up = sb("iota_up", [P, UNITS], f32, setup)
                iota_down = sb("iota_down", [P, UNITS], f32, setup)
                reach = sb("reach", [WINDOWS, 2, UNITS], f32, setup)
            diag = sb("diag", [P, NT, P], f32, early)
            junk = sb("junk", [P, 2, H2], f32, early)
            dots = sb("dots", [P, 4 * NT], f32, early)
            a_bc = sb("a_bc", [P, 2 * D], f32, early)
            with ExitStack() as first:
                xT_raw = sb("xT_raw", [P, KT, N], f32, first)
            att = sb("att", [P, NT, NP], f32, early)

        with ExitStack() as late:
            x1_hi = sb("x1_hi", [P, NT, D], f32r, late)
            x1_lo = sb("x1_lo", [P, NT, D], f32r, late)
            u = sb("u", [P, NT, D], f32, late)
            bias_bc = sb("bias_bc", [P, D], f32, late)
            bg_bc = sb("bg_bc", [P, D], f32, late)
            with ExitStack() as elu:
                gt = [sb(f"gt{b}", [P, D], f32, elu) for b in range(2)]
                et = [sb(f"et{b}", [P, D], f32, elu) for b in range(2)]
            with ExitStack() as agg:
                C_hi = sb("C_hi", [P, NT, NP], f32r, agg)
                sb("under_elu", [P, NT, NP], f32, agg)
                c16 = sb("c16", [P, NT, NP], i16, agg)
            with ExitStack() as final:
                xf = sb("xf", [P, NT, D], f32, final)
                zt = [sb(f"zt{b}", [P, H2], f32, final) for b in range(2)]

        ps = ctx.enter_context(nc.psum_tensor("ps", [P, 8 * H2], f32))

        def bank(b, p=P, c0=0, c=H2):
            return ps[0:p, b * H2 + c0:b * H2 + c0 + c]

        def pair(b, p=P):
            return ps[0:p, 2 * b * H2:2 * (b + 1) * H2]

        edges_here = sem("edges_here")
        xT_here = [sem(f"xT_here{k}") for k in range(KT)]
        a_here = sem("a_here")
        bias_here = sem("bias_here")
        x_here = sem("x_here")
        raw_here = [sem(f"raw_here{b}") for b in range(RING)]
        w_hi_done = sem("w_hi_done")
        w_lo_done = sem("w_lo_done")
        w_used = sem("w_used")
        pool_consts = sem("pool_consts")
        pool_step = sem("pool_step")
        dve_step = sem("dve_step")
        act_step = sem("act_step")
        consts_done = sem("consts_done")
        units_diag_done = sem("units_diag_done")
        units_bcast = sem("units_bcast")
        lohi_done = sem("lohi_done")
        lohi_turned = sem("lohi_turned")
        row_done = sem("row_done")
        built = sem("built")
        slot_free = sem("slot_free")
        window_counted = sem("window_counted")
        window_copied = sem("window_copied")
        turned = sem("turned")
        turned_read = sem("turned_read")
        flushed = sem("flushed")
        summed = sem("summed")
        xT_hi_done = sem("xT_hi_done")
        xT_lo_done = sem("xT_lo_done")
        u_ready = sem("u_ready")
        u_drained = sem("u_drained")
        h_hi_done = sem("h_hi_done")
        diag_done = sem("diag_done")
        ar_bcast = sem("ar_bcast")
        sum_done = sem("sum_done")
        leaky_done = sem("leaky_done")
        exp_done = sem("exp_done")
        att_done = sem("att_done")
        attT_ready = sem("attT_ready")
        attT_hi_done = sem("attT_hi_done")
        attT_lo_done = sem("attT_lo_done")
        hp_ready = sem("hp_ready")
        rowsum_done = sem("rowsum_done")
        hp_read = sem("hp_read")
        elu_exp = sem("elu_exp")
        y_done = sem("y_done")
        std_done = sem("std_done")
        x1_done = sem("x1_done")
        x1_hi_done = sem("x1_hi_done")
        x1_lo_done = sem("x1_lo_done")
        x1T_ready = sem("x1T_ready")
        x1T_hi_done = sem("x1T_hi_done")
        x1T_lo_done = sem("x1T_lo_done")
        u_init = sem("u_init")
        c16_here = sem("c16_here")
        C_ready = sem("C_ready")
        g_ready = sem("g_ready")
        g_drained = sem("g_drained")
        scale_ready = sem("scale_ready")
        sum_hi_done = sem("sum_hi_done")
        xt2_ready = sem("xt2_ready")
        xt2_hi_done = sem("xt2_hi_done")
        xt2_lo_done = sem("xt2_lo_done")
        uT_ready = sem("uT_ready")
        uT_hi_done = sem("uT_hi_done")
        uT_lo_done = sem("uT_lo_done")
        tanh_done = sem("tanh_done")
        xf_done = sem("xf_done")
        d_done = sem("d_done")
        var_done = sem("var_done")
        std2_done = sem("std2_done")
        y2_done = sem("y2_done")
        out_done = sem("out_done")

        SEG_W = 0
        SEG_U = 2
        SEG_G = SEG_U + 2 * STEPS
        SEGS = SEG_G + 4
        BANKS_G = NT * (SEG_G)

        def chunk_rows(n, k):
            if n < SEG_G:
                return (n // 2) * D + k * P, (n % 2) * H2
            m = n - SEG_G
            return (STEPS + 1 + (1 - m % 2)) * D + k * P, (m // 2) * H2

        def closes(n):
            return not isinstance(n, int) or n < SEG_G or n % 2 == 1

        def used_before(n):
            if not isinstance(n, int) or n < SEG_G:
                return n * (KT - 1)
            return SEG_G * (KT - 1) + (n - SEG_G) * KT - (n - SEG_G) // 2

        def filled(n):
            if not isinstance(n, int) or n < SEG_G:
                return n * NT + NT
            return BANKS_G + NT * ((n - SEG_G) // 2 + 1)

        def items(v):
            return [divmod(i, NT) for i in range(v * KT * NT // HALF_W, (v + 1) * KT * NT // HALF_W)]

        def chunk_ends(v):
            return [k for k, t in items(v) if t == NT - 1]

        PE_ENGINE, DVE_ENGINE = mybir.EngineType.PE, mybir.EngineType.DVE

        def window_range(engine, w):
            why = "a count of units of the edge list, worked out above"
            return [nc.values_load(lohi_row[0:1, ds(w + c * WINDOWS, 1)], engines=(engine,), min_val=c, max_val=UNITS - 1 + c,
                                   skip_runtime_bounds_check_because=why) for c in range(2)]

        block = ctx.enter_context(nc.Block())

        @block.sync
        def _(sp):
            def load_chunk(n, k, at=None, first=False):
                if not first:
                    sp.wait_ge(w_lo_done, 8 * n + k - RING + 1)
                r0, c0 = at or chunk_rows(n, k)
                sp.dma_start(w_raw[k % RING][:, :], weights[ds(r0, P), c0:c0 + H2]).then_inc(raw_here[k % RING], 16)

            def load_ahead(n, last=False):
                for k in range(KT):
                    if k < KT - RING:
                        load_chunk(n, k + RING)
                    elif not last:
                        load_chunk(n + 1, k + RING - KT)

            sp.dma_start(ints[:, 0, :], dst_cols).then_inc(edges_here, 16)
            sp.dma_start(ints[:, 1, :], src_cols).then_inc(edges_here, 16)
            sp.dma_start(ints[:, 2, :], type_cols).then_inc(edges_here, 16)
            sp.dma_start(units_i[:, :], dst_units).then_inc(edges_here, 16)
            for k in range(KT):
                if k < RING:
                    load_chunk(0, k, first=True)
                sp.dma_start(xT_raw[:, k, :], xT[k * P:(k + 1) * P, :]).then_inc(xT_here[k], 16)
            sp.dma_start(a_bc[:, :], a[0, :].partition_broadcast(P)).then_inc(a_here, 16)
            load_ahead(0)
            load_ahead(1)
            sp.wait_ge(turned_read, 2 * WINDOWS + 1)
            for m in range(NT):
                sp.dma_start(counts_dram[:, m, :, :].rearrange("r p n -> p r n"), counts[:, m, :, :]).then_inc(flushed, 16)
            sp.wait_ge(attT_lo_done, NT)
            sp.wait_ge(flushed, 16 * NT)
            sp.dma_start(u[:, 0:NT - 1, :], x[0:P * (NT - 1), :].rearrange("(t p) d -> p t d", p=P)).then_inc(x_here, 16)
            sp.dma_start(u[0:rows(NT - 1), NT - 1, :], x[P * (NT - 1):N, :]).then_inc(x_here, 16)
            sp.dma_start(bias_bc[:, :], bias.partition_broadcast(P)).then_inc(bias_here, 16)
            sp.dma_start(bg_bc[:, :], b_gate.partition_broadcast(P)).then_inc(bias_here, 16)
            sp.dma_start(c16[:, :, :], counts_dram[0, :, :, :].rearrange("m p n -> p m n")).then_inc(c16_here, 16)

            def step_loads(i, last):
                for h in range(2):
                    n = 2 * i + SEG_U + h
                    for k in range(KT - RING):
                        load_chunk(n, k + RING, at=((i + 1) * D + (k + RING) * P, h * H2))
                    for k in range(RING):
                        load_chunk(n + 1, k, at=((i + 1 + h) * D + k * P, (1 - h) * H2))
                if not last:
                    sp.wait_ge(C_ready, i + 1)
                    sp.dma_start(c16[:, :, :], counts_dram[ds(i + 1, 1), :, :, :].rearrange("o m p n -> p (o m) n"))\
                      .then_inc(c16_here, 16)

            with sp.Fori(0, R // 2 - 1) as j:
                for s in range(2):
                    step_loads(2 * j + s, False)
            step_loads(R - 2, False)
            step_loads(R - 1, True)
            for n in range(SEG_U + 2 * R, SEGS):
                load_ahead(n, last=n == SEGS - 1)
            for t in range(NT):
                sp.wait_ge(y2_done, t + 1)
                sp.dma_start(out[t * P:t * P + rows(t), :], u[0:rows(t), t, :]).then_inc(out_done, 16)
            sp.wait_ge(out_done, 16 * NT)

        @block.gpsimd
        def _(pool):
            steps = [0]

            def step(ins):
                steps[0] += 1
                ins.then_inc(pool_step, 1)
                pool.wait_ge(pool_step, steps[0])

            pool.iota(iota_i[:, :], pattern=[[1, NP]], base=0, channel_multiplier=0).then_inc(pool_consts, 1)
            pool.iota(part_col[:, :], pattern=[[0, 1]], base=0, channel_multiplier=1,
                      allow_small_or_imprecise_dtypes=True).then_inc(pool_consts, 1)
            pool.iota(iota_up[:, :], pattern=[[1, UNITS]], base=1, channel_multiplier=0,
                      allow_small_or_imprecise_dtypes=True).then_inc(pool_consts, 1)
            pool.iota(iota_down[:, :], pattern=[[-1, UNITS]], base=1000, channel_multiplier=0,
                      allow_small_or_imprecise_dtypes=True).then_inc(pool_consts, 1)
            pool.iota(iota_q[:, :], pattern=[[1, P]], base=0, channel_multiplier=0,
                      allow_small_or_imprecise_dtypes=True).then_inc(pool_consts, 1)

            def split_chunk(n, k):
                pool.wait_ge(w_hi_done, 8 * n + k + 1)
                pool.tensor_tensor(w_lo[k % RING][:, :], w_raw[k % RING][:, :], w_hi[k % RING][:, :].bitcast(f32),
                                   ALU.subtract).then_inc(w_lo_done, 1)

            def split_ahead(n, last=False):
                for k in range(KT):
                    if k < KT - RING:
                        split_chunk(n, k + RING)
                    elif not last:
                        split_chunk(n + 1, k + RING - KT)

            def add_relations(half, v):
                pool.wait_ge(turned_read, 2 * (HALF_W * half + v + 1) + 1)
                cols = ds((HALF_W * half + v + 1 - SUM_W) * WIN, SUM_W * WIN)
                n = [(v + 1) // SUM_W * 2 * R - 2 * R]

                def ordered(ins):
                    n[0] += 1
                    ins.then_inc(summed, 1)
                    pool.wait_ge(summed, (HALF_W // SUM_W * 2 * R) * half + n[0])

                ordered(pool.tensor_copy(count_sum[:, :, :], counts[:, :, 0, cols]))
                for r in range(1, R):
                    ordered(pool.tensor_copy(count_f[:, :, :], counts[:, :, r, cols]))
                    ordered(pool.tensor_tensor(count_sum[:, :, :], count_sum[:, :, :], count_f[:, :, :], ALU.add))
                ordered(pool.tensor_copy(counts_all[:, :, cols], count_sum[:, :, :]))

            for k in range(KT):
                if k < RING:
                    split_chunk(0, k)
                pool.wait_ge(xT_hi_done, k + 1)
                pool.tensor_tensor(M_lo[0][:, k, 0:N], xT_raw[:, k, :], M_hi[0][:, k, 0:N].bitcast(f32),
                                   ALU.subtract).then_inc(xT_lo_done, 1)
            with pool.Fori(0, 2) as half:
                for v in range(HALF_W):
                    for k in chunk_ends(v):
                        split_chunk(half + (k + RING) // KT, (k + RING) % KT)
                    if v % SUM_W == SUM_W - 1:
                        add_relations(half, v)
            for t in range(NT):
                pool.wait_ge(x1_hi_done, t + 1)
                pool.tensor_tensor(x1_lo[0:rows(t), t, :], u[0:rows(t), t, :], x1_hi[0:rows(t), t, :].bitcast(f32),
                                   ALU.subtract).then_inc(x1_lo_done, 1)

            with pool.Fori(0, R // 2) as j:
                for half in range(4):
                    split_ahead(4 * j + SEG_U + half)
            split_ahead(SEG_U + 2 * R)
            split_ahead(SEG_U + 2 * R + 1)
            split_ahead(SEG_G)
            for t in range(NT):
                r = slice(0, rows(t))
                if t == 0:
                    pool.wait_ge(g_drained, ITEMS + ITEMS * R)
                pool.tensor_tensor(xf[r, t, :], x1_hi[r, t, :].bitcast(f32), x1_lo[r, t, :].bitcast(f32), ALU.add)\
                    .then_inc(xf_done, 1)
            split_ahead(SEG_G + 1)
            for t in range(NT):
                r = slice(0, rows(t))
                pool.wait_ge(tanh_done, t + 1)
                pool.wait_ge(xf_done, t + 1)
                pool.tensor_tensor(u[r, t, :], u[r, t, :], xf[r, t, :], ALU.subtract).then_inc(d_done, 1)
            split_ahead(SEG_G + 2)
            split_ahead(SEG_G + 3, last=True)

        @block.scalar
        def _(act):
            act.sem_inc(window_copied, 1)
            act.sem_inc(turned_read, 1)

            def split_chunk(n, k, first=False):
                act.wait_ge(raw_here[k % RING], 32 * n + 16 * (k // RING) + 16)
                if not first:
                    m, j = (n, k - RING) if k >= RING else (n - 1, k + KT - RING)
                    if closes(m) and j == KT - 1:
                        act.wait_ge(u_ready, filled(m))
                    else:
                        act.wait_ge(w_used, used_before(m) + j + 1)
                nc.scalar.copy(w_hi[k % RING][:, :], w_raw[k % RING][:, :]).then_inc(w_hi_done, 1)

            def split_ahead(n, last=False):
                for k in range(KT):
                    if k < KT - RING:
                        split_chunk(n, k + RING)
                    elif not last:
                        split_chunk(n + 1, k + RING - KT)

            for k in range(KT):
                if k < RING:
                    split_chunk(0, k, first=True)
                act.wait_ge(xT_here[k], 16)
                nc.scalar.copy(M_hi[0][:, k, 0:N], xT_raw[:, k, :]).then_inc(xT_hi_done, 1)

            def place(w, part):
                blocks = [(0, NT - 1), (NT - 1, NT)][part]
                act.wait_ge(turned, 2 * w + part + 1)
                nc.scalar.copy(counts[:, blocks[0]:blocks[1], :, ds(WIN * w, WIN)],
                               bank(7, c=(blocks[1] - blocks[0]) * P).rearrange("p (m d r) -> p m r d", d=WIN, r=R))\
                  .then_inc(turned_read, 1)

            with act.Fori(0, 2) as half:
                for v in range(HALF_W):
                    w = HALF_W * half + v
                    act.wait_ge(window_counted, w + 1)
                    nc.scalar.copy(win_sb[v % 2][:, :].rearrange("p (b n) -> p b n", b=2),
                                   ps[:, 5 * H2:7 * H2].rearrange("p (b n) -> p b n", b=2)[:, :, 0:SPLIT])\
                      .then_inc(window_copied, 1)
                    if v:
                        place(w - 1, 1)
                    place(w, 0)
                    if v == HALF_W - 1:
                        place(w, 1)
                    for k in chunk_ends(v):
                        split_chunk(half + (k + RING) // KT, (k + RING) % KT)
                for t in range(NT):
                    act.wait_ge(u_ready, NT * half + t + 1)
                    nc.scalar.copy(h_part(0, half, t, rows(t)), bank(t, rows(t))).then_inc(h_hi_done, 1)
            act.wait_ge(ar_bcast, 1)
            act.wait_ge(diag_done, 1)
            for t in range(NT):
                nc.scalar.activation(att[0:rows(t), t, :].rearrange("p (b n) -> p b n", b=2),
                                     ps[0:rows(t), 5 * H2:7 * H2].rearrange("p (b n) -> p b n", b=2)[:, :, 0:SPLIT],
                                     ACT.Identity, bias=alr[0:rows(t), t:t + 1]).then_inc(sum_done, 1)
            for t in range(NT):
                act.wait_ge(leaky_done, t + 1)
                nc.scalar.activation(att[0:rows(t), t, :], att[0:rows(t), t, :], ACT.Exp, scale=-1.0).then_inc(exp_done, 1)
            for t in range(NT):
                act.wait_ge(attT_ready, t + 1)
                nc.scalar.copy(M_hi[0][0:rows(t), t, 0:N], pair(t % 3, rows(t))[:, 0:N]).then_inc(attT_hi_done, 1)
            for t in range(NT):
                act.wait_ge(hp_ready, t + 1)
                if t >= 2:
                    act.wait_ge(y_done, t - 1)
                if t == 0:
                    act.wait_ge(rowsum_done, 1)
                nc.scalar.activation(et[t % 2][0:rows(t), :], pair(t % 3, rows(t)), ACT.Exp, scale=rowsum[0:rows(t), t:t + 1])\
                  .then_inc(elu_exp, 1)
                nc.scalar.activation(gt[t % 2][0:rows(t), :], pair(t % 3, rows(t)), ACT.Relu, scale=rowsum[0:rows(t), t:t + 1])\
                  .then_inc(hp_read, 1)
            act.wait_ge(y_done, NT)
            nc.scalar.activation(rstd[:, :], mv[:, :, 1], ACT.Sqrt, bias=eps_col[:, :]).then_inc(std_done, 1)
            for t in range(NT):
                act.wait_ge(x1_done, t + 1)
                nc.scalar.copy(x1_hi[0:rows(t), t, :], u[0:rows(t), t, :]).then_inc(x1_hi_done, 1)
                act.wait_ge(x1T_ready, t + 1)
                nc.scalar.copy(M_hi[0][:, :, t * P:t * P + rows(t)],
                               pair(t % 3).rearrange("p (k n) -> p k n", k=KT)[:, :, 0:rows(t)]).then_inc(x1T_hi_done, 1)

            def sums_high(i, odd, half):
                for e in range(half * SUMS // 2, (half + 1) * SUMS // 2):
                    c0, cn = NCOL[e % 2]
                    act.wait_ge(g_ready, ITEMS * i + e + 2)
                    nc.scalar.copy(M_hi[1 - odd][:, e // 2, c0:c0 + cn], bank(5 + (e + 1) % GB, c=cn)).then_inc(sum_hi_done, 1)

            def step_work(i, odd):
                for half in range(2):
                    split_ahead(2 * i + SEG_U + half)
                    sums_high(i, odd, half)

            with act.Fori(0, R // 2) as j:
                for s in range(2):
                    step_work(2 * j + s, s)

            for half in range(2):
                split_ahead(SEG_U + 2 * R + half)
                for t, kh in [(t, kh) for t in range(NT) for kh in range(2)][half * NT:(half + 1) * NT]:
                    act.wait_ge(xt2_ready, 2 * (2 * t + kh) + 1)
                    nc.scalar.copy(M_hi[1][:, 4 * kh:4 * kh + 4, t * P:t * P + rows(t)],
                                   bank(5 + 2 * (2 * t + kh) % GB).rearrange("p (k n) -> p k n", k=4)[:, :, 0:rows(t)])\
                      .then_inc(xt2_hi_done, 1)
            split_ahead(SEG_G)
            for t in range(NT):
                for kh in range(2):
                    it = 2 * t + kh
                    act.wait_ge(uT_ready, it + 1)
                    nc.scalar.copy(M_hi[0][:, 4 * kh:4 * kh + 4, t * P:t * P + rows(t)],
                                   bank(5 + it % GB).rearrange("p (k n) -> p k n", k=4)[:, :, 0:rows(t)])\
                      .then_inc(uT_hi_done, 1)
            split_ahead(SEG_G + 1)
            for t in range(NT):
                nc.scalar.activation(u[0:rows(t), t, :], u[0:rows(t), t, :], ACT.Tanh).then_inc(tanh_done, 1)
            split_ahead(SEG_G + 2)
            split_ahead(SEG_G + 3, last=True)
            for t in range(NT):
                act.wait_ge(var_done, t + 1)
                nc.scalar.activation(rstd[0:rows(t), t:t + 1], mv[0:rows(t), t, 1:2], ACT.Sqrt,
                                     bias=eps_col[0:rows(t), :]).then_inc(std2_done, 1)

        @block.vector
        def _(dve):
            steps = [0]

            def step(ins):
                steps[0] += 1
                ins.then_inc(dve_step, 1)
                dve.wait_ge(dve_step, steps[0])

            v = nc.vector
            dve.sem_inc(u_drained, NT)
            dve.sem_inc(built, PAIR - 1)
            dve.sem_inc(g_drained, ITEMS)
            v.memset(ones[:, :], 1.0)
            v.memset(zeros[:, :], 0.0)
            v.memset(ones_r[:, :].bitcast(f32), 1.0)
            v.memset(eps_col[:, :], EPS)
            v.memset(rowsum[:, :], 1.0)
            v.memset(mv[:, :, :], 1.0)
            v.memset(scale[0][:, :], 1.0)
            step(v.memset(dots[:, :], 0.0))
            dve.wait_ge(pool_consts, 5)
            step(v.tensor_copy(iota_node[:, :], iota_i[:, :]))
            step(v.tensor_scalar(ident[:, :], iota_node[:, 0:P], part_col[:, :], None, ALU.is_equal))
            v.tensor_scalar(win_edge[:, 0:1], part_col[:, :], float(WIN), None, ALU.mult)
            step(v.tensor_scalar(win_edge[:, 1:2], part_col[:, :], float(WIN), float(WIN - 1), ALU.mult, ALU.add))
            dve.wait_ge(edges_here, 64)
            v.tensor_reduce(unit_mm[:, 0:1], units_i[:, :], X, ALU.max)
            step(v.tensor_reduce(unit_mm[:, 1:2], units_i[:, :], X, ALU.min))
            for c in range(2):
                d = v.tensor_scalar(unit_diag[:, c, 0:UNITS], ident[0:UNITS, 0:UNITS], unit_mm[:, c:c + 1], None, ALU.mult)
            d.then_inc(units_diag_done, 1)
            v.tensor_copy(src_f[:, :], ints[:, 1, :])
            step(v.tensor_copy(q_f[:, :], ints[:, 0, :]))
            step(v.tensor_copy(type_f[:, :], ints[:, 2, :]))
            step(v.scalar_tensor_tensor(q_f[:, :], q_f[:, :], float(R), type_f[:, :], ALU.mult, ALU.add))
            dve.wait_ge(units_bcast, 1)
            step(v.scalar_tensor_tensor(reach[:, 0, :], ps[0:WINDOWS, 4 * H2:4 * H2 + UNITS], win_edge[0:WINDOWS, 0:1],
                                        iota_down[0:WINDOWS, :], ALU.is_ge, ALU.mult))
            step(v.scalar_tensor_tensor(reach[:, 1, :], ps[0:WINDOWS, 5 * H2:5 * H2 + UNITS], win_edge[0:WINDOWS, 1:2],
                                        iota_up[0:WINDOWS, :], ALU.is_le, ALU.mult))
            step(v.tensor_reduce(lohi[:, 0:2], reach[:, :, :], X, ALU.max))
            step(v.tensor_scalar(lohi[:, 2:3], lohi[:, 0:1], -1.0, 1000.0, ALU.mult, ALU.add))
            v.tensor_scalar(lohi[:, 3:4], lohi[:, 2:3], 1.0, lohi[:, 1:2], ALU.add, ALU.max).then_inc(lohi_done, 1)
            dve.wait_ge(lohi_turned, 1)
            v.tensor_copy(lohi_row[:, 0:WINDOWS], ps[0:1, 6 * H2:6 * H2 + WINDOWS])
            v.tensor_copy(lohi_row[:, WINDOWS:2 * WINDOWS], ps[0:1, 7 * H2:7 * H2 + WINDOWS]).then_inc(row_done, 1)
            dve.wait_ge(row_done, 1)

            turn = dve.alloc_register("dve_turn")
            dve.reg_mov(turn, 0)
            with dve.Fori(0, 2) as half:
                for v_ in range(HALF_W):
                    w = HALF_W * half + v_
                    lo, hi = window_range(DVE_ENGINE, w)
                    with dve.Fori(lo, hi) as unit:
                        dve.reg_add(turn, turn, 1)
                        n = dve.snap(turn, min_val=1, max_val=WINDOWS * UNITS)
                        at = dve.snap((n % DEPTH) * HOT)
                        tile = dve.snap(unit * PAIR)
                        dve.wait_ge(slot_free, n)
                        for s in range(PAIR):
                            v.tensor_scalar(hot[:, ds(at + s * NP, NP)], iota_node[:, :], src_f[:, ds(tile + s, 1)], None,
                                            ALU.is_equal)
                            v.tensor_scalar(hot[:, ds(at + PAIR * NP + s * P, P)], iota_q[:, :], float(P * v_),
                                            q_f[:, ds(tile + s, 1)], ALU.add, ALU.is_equal).then_inc(built, 1)
                v.tensor_scalar(iota_q[:, :], iota_q[:, :], float(P * HALF_W), None, ALU.add)
                for t in range(NT):
                    r = slice(0, rows(t))
                    dve.wait_ge(h_hi_done, NT * half + t + 1)
                    if t == 0:
                        dve.wait_ge(a_here, 16)
                    for lr in range(2):
                        v.scalar_tensor_tensor(junk[r, lr, :], bank(t, rows(t)), 1.0, a_bc[r, ds(half * H2 + lr * D, H2)],
                                               ALU.mult, ALU.mult, accum_out=dots[r, ds(half * 2 * NT + lr * NT + t, 1)])
                    v.tensor_tensor(h_part(1, half, t, rows(t)), bank(t, rows(t)), h_part(0, half, t, rows(t)).bitcast(f32),
                                    ALU.subtract).then_inc(u_drained, 1)
                    dve.wait_ge(u_drained, NT * half + t + 1 + NT)
            step(v.tensor_tensor(alr[:, :], dots[:, 0:2 * NT], dots[:, 2 * NT:4 * NT], ALU.add))
            for t in range(NT):
                d = v.tensor_scalar(diag[:, t, :], ident[:, :], alr[:, NT + t:NT + t + 1], None, ALU.mult)
            d.then_inc(diag_done, 1)
            for t in range(NT):
                r = slice(0, rows(t))
                dve.wait_ge(sum_done, t + 1)
                v.scalar_tensor_tensor(att[r, t, :], att[r, t, :], SLOPE, att[r, t, :], ALU.mult, ALU.max)\
                    .then_inc(leaky_done, 1)
            dve.wait_ge(summed, 2 * HALF_W // SUM_W * 2 * R)
            for t in range(NT):
                r = slice(0, rows(t))
                dve.wait_ge(exp_done, t + 1)
                v.scalar_tensor_tensor(att[r, t, :], att[r, t, :], FLT_MAX, counts_all[r, t, :], ALU.min, ALU.mult,
                                       accum_out=rowsum[r, t:t + 1]).then_inc(att_done, 1)
            dve.wait_ge(att_done, NT)
            step(v.tensor_scalar(rowsum[:, :], rowsum[:, :], EPS, None, ALU.add))
            v.reciprocal(rowsum[:, :], rowsum[:, :]).then_inc(rowsum_done, 1)
            for t in range(NT):
                r = slice(0, rows(t))
                dve.wait_ge(attT_hi_done, t + 1)
                v.tensor_tensor(M_lo[0][r, t, 0:N], pair(t % 3, rows(t))[:, 0:N], M_hi[0][r, t, 0:N].bitcast(f32),
                                ALU.subtract).then_inc(attT_lo_done, 1)
            dve.wait_ge(x_here, 32)

            def add_elu(t):
                r = slice(0, rows(t))
                dve.wait_ge(elu_exp, t + 1)
                dve.wait_ge(hp_read, t + 1)
                step(v.scalar_tensor_tensor(gt[t % 2][r, :], et[t % 2][r, :], 1.0, gt[t % 2][r, :], ALU.min, ALU.add))
                step(v.scalar_tensor_tensor(u[r, t, :], gt[t % 2][r, :], -1.0, u[r, t, :], ALU.add, ALU.add))
                for c in range(2):
                    s_ = v.bn_stats(stats[r, t % 2, c, :], u[r, t, c * H2:(c + 1) * H2])
                step(s_)
                v.bn_aggr(mv[r, t, :], stats[r, t % 2, :, :]).then_inc(y_done, 1)

            for t in range(NT):
                add_elu(t)
            dve.wait_ge(std_done, 1)
            step(v.reciprocal(rstd[:, :], rstd[:, :]))
            for t in range(NT):
                r = slice(0, rows(t))
                v.tensor_scalar(u[r, t, :], u[r, t, :], mv[r, t, 0:1], rstd[r, t:t + 1], ALU.subtract, ALU.mult)\
                    .then_inc(x1_done, 1)
            for t in range(NT):
                dve.wait_ge(x1T_hi_done, t + 1)
                v.tensor_tensor(M_lo[0][:, :, t * P:t * P + rows(t)],
                                pair(t % 3).rearrange("p (k n) -> p k n", k=KT)[:, :, 0:rows(t)],
                                M_hi[0][:, :, t * P:t * P + rows(t)].bitcast(f32), ALU.subtract).then_inc(x1T_lo_done, 1)
            dve.wait_ge(x1_lo_done, NT)
            dve.wait_ge(bias_here, 32)
            for t in range(NT):
                d = v.tensor_copy(u[:, t, :], bias_bc[:, :])
            d.then_inc(u_init, 1)
            dve.wait_ge(u_init, 1)

            def convert_counts(i):
                dve.wait_ge(c16_here, 16 * i + 16)
                v.tensor_copy(C_hi[:, :, :], c16[:, :, :]).then_inc(C_ready, 1)

            def add_u(i, odd, half, t):
                r = slice(0, rows(t))
                if t == 0 and half == 0 and not (isinstance(i, int) and i == 0):
                    dve.wait_ge(scale_ready, i + 1)
                dve.wait_ge(u_ready, 2 * NT * i + NT * (SEG_U + half) + t + 1)
                v.scalar_tensor_tensor(u[r, t, half * H2:(half + 1) * H2], bank(t, rows(t)), scale[odd][r, t:t + 1],
                                       u[r, t, half * H2:(half + 1) * H2], ALU.mult, ALU.add).then_inc(u_drained, 1)

            def invert(i, odd):
                dve.wait_ge(g_ready, ITEMS * i + 1)
                v.tensor_scalar(scale[1 - odd][:, :], bank(5, c=2 * NT).rearrange("p (t c) -> p t c", c=2)[:, :, 0],
                                1.0, None, ALU.max).then_inc(g_drained, 1)
                dve.wait_ge(g_drained, ITEMS * (i + 1) + 1)
                v.reciprocal(scale[1 - odd][:, :], scale[1 - odd][:, :]).then_inc(scale_ready, 1)

            def sum_low(i, odd, e):
                c0, cn = NCOL[e % 2]
                dve.wait_ge(sum_hi_done, SUMS * i + e + 1)
                v.tensor_tensor(M_lo[1 - odd][:, e // 2, c0:c0 + cn], bank(5 + (e + 1) % GB, c=cn),
                                M_hi[1 - odd][:, e // 2, c0:c0 + cn].bitcast(f32), ALU.subtract).then_inc(g_drained, 1)

            def step_work(i, odd):
                convert_counts(i)
                for half in range(2):
                    add_u(i, odd, half, 0)
                    if half == 0:
                        invert(i, odd)
                    for n in range(SUMS // 2):
                        sum_low(i, odd, half * SUMS // 2 + n)
                        if n < NT - 1:
                            add_u(i, odd, half, n + 1)

            dve.sem_inc(scale_ready, 1)
            with dve.Fori(0, R // 2) as j:
                for s in range(2):
                    step_work(2 * j + s, s)

            for half in range(2):
                for t in range(NT):
                    add_u(R, 0, half, t)
                for t, kh in [(t, kh) for t in range(NT) for kh in range(2)][half * NT:(half + 1) * NT]:
                    it = 2 * (2 * t + kh) + 1
                    dve.wait_ge(xt2_ready, it + 1)
                    v.tensor_copy(M_lo[1][:, 4 * kh:4 * kh + 4, t * P:t * P + rows(t)],
                                  bank(5 + it % GB).rearrange("p (k n) -> p k n", k=4)[:, :, 0:rows(t)])\
                        .then_inc(xt2_lo_done, 1)
            for t in range(NT):
                for kh in range(2):
                    it = 2 * t + kh
                    dve.wait_ge(uT_hi_done, it + 1)
                    v.tensor_tensor(M_lo[0][:, 4 * kh:4 * kh + 4, t * P:t * P + rows(t)],
                                    bank(5 + it % GB).rearrange("p (k n) -> p k n", k=4)[:, :, 0:rows(t)],
                                    M_hi[0][:, 4 * kh:4 * kh + 4, t * P:t * P + rows(t)].bitcast(f32), ALU.subtract)\
                        .then_inc(uT_lo_done, 1)
            for half in range(2):
                for t in range(NT):
                    r, c = slice(0, rows(t)), slice(half * H2, (half + 1) * H2)
                    z = zt[t % 2]
                    dve.wait_ge(u_ready, BANKS_G + NT * half + t + 1)
                    v.tensor_tensor(z[r, :], bank(t, rows(t)), bg_bc[r, c], ALU.add).then_inc(u_drained, 1)
                    dve.wait_ge(u_drained, BANKS_G + NT * half + t + 1 + NT)
                    dve.wait_ge(d_done, t + 1)
                    step(v.tensor_tensor(z[r, :], z[r, :], u[r, t, c], ALU.mult))
                    step(v.scalar_tensor_tensor(u[r, t, c], xf[r, t, c], 2.0, z[r, :], ALU.mult, ALU.add))
                    if half:
                        for hh in range(2):
                            s_ = v.bn_stats(stats[r, t % 2, hh, :], u[r, t, hh * H2:(hh + 1) * H2])
                        step(s_)
                        v.bn_aggr(mv[r, t, :], stats[r, t % 2, :, :]).then_inc(var_done, 1)
            for t in range(NT):
                r = slice(0, rows(t))
                dve.wait_ge(std2_done, t + 1)
                step(v.reciprocal(rstd[r, t:t + 1], rstd[r, t:t + 1]))
                v.tensor_scalar(u[r, t, :], u[r, t, :], mv[r, t, 0:1], rstd[r, t:t + 1], ALU.subtract, ALU.mult)\
                    .then_inc(y2_done, 1)

        @block.tensor
        def _(pe):
            mm = nc.tensor.matmul
            pe.sem_inc(slot_free, DEPTH)

            pe.wait_ge(units_diag_done, 1)
            for c in range(2):
                last = mm(ps[0:WINDOWS, (4 + c) * H2:(4 + c) * H2 + UNITS], ones[0:UNITS, 0:WINDOWS],
                          unit_diag[:, c, 0:UNITS], start=True, stop=True)
            last.then_inc(units_bcast, 1)
            pe.wait_ge(lohi_done, 1)
            for c in range(2):
                last = mm(ps[0:1, (6 + c) * H2:(6 + c) * H2 + WINDOWS], lohi[:, 2 + c:3 + c],
                          ident[0:WINDOWS, 0:WINDOWS], start=True, stop=True)
            last.then_inc(lohi_turned, 1)

            pe.wait_ge(row_done, 1)
            turn = pe.alloc_register("pe_turn")
            pe.reg_mov(turn, 0)
            def product_item(k, t, lhs_hi, lhs_lo, opens, closes_):
                c = slice(t * P, t * P + rows(t))
                o = bank(t, rows(t))
                mm(o, lhs_hi[:, k, c], w_hi[k % RING][:, :], start=opens, stop=False)
                mm(o, lhs_lo[:, k, c], w_hi[k % RING][:, :], start=False, stop=False)
                last = mm(o, lhs_hi[:, k, c], w_lo[k % RING][:, :], start=False, stop=closes_)
                if closes_:
                    last.then_inc(u_ready, 1)
                elif t == NT - 1:
                    last.then_inc(w_used, 1)

            def turn_back(w, v, part):
                pe.wait_ge(turned_read, 2 * w + part + 1)
                if part == 0:
                    pe.wait_ge(window_copied, w + 2)
                for j, m in enumerate(range(NT - 1) if part == 0 else [NT - 1]):
                    last = nc.tensor.transpose(bank(7, c0=j * P, c=P), win_sb[v % 2][:, m * P:(m + 1) * P], ident[:, :])
                last.then_inc(turned, 1)

            with pe.Fori(0, 2) as half:
                for v in range(HALF_W):
                    w = HALF_W * half + v
                    lo, hi = window_range(PE_ENGINE, w)
                    pe.wait_ge(window_copied, w + 1)
                    for c in range(2):
                        mm(bank(5 + c, c=2), zeros[:, :], zeros[:, 0:2], start=True, stop=False, skip_group_check=True)
                    with pe.Fori(lo, hi) as unit:
                        pe.reg_add(turn, turn, 1)
                        n = pe.snap(turn, min_val=1, max_val=WINDOWS * UNITS)
                        at = pe.snap((n % DEPTH) * HOT)
                        for s in range(PAIR):
                            pe.wait_ge(built, n * PAIR + s)
                            for c in range(2):
                                last = mm(bank(5 + c, c=SPLIT), hot[:, ds(at + PAIR * NP + s * P, P)],
                                          hot[:, ds(at + s * NP + c * SPLIT, SPLIT)],
                                          start=False, stop=False, skip_group_check=True)
                        last.then_inc(slot_free, 1)
                    for c in range(2):
                        last = mm(bank(5 + c, c=2), zeros[:, :], zeros[:, 0:2], start=False, stop=True,
                                  skip_group_check=True)
                    last.then_inc(window_counted, 1)
                    if v:
                        turn_back(w - 1, v - 1, 1)
                    for k, t in items(v):
                        if t == 0:
                            pe.wait_ge(w_lo_done, 8 * half + k + 1)
                            pe.wait_ge(xT_lo_done, k + 1)
                        if k == 0:
                            pe.wait_ge(u_drained, NT * half + t + 1)
                        product_item(k, t, M_hi[0], M_lo[0], k == 0, k == KT - 1)
                    turn_back(w, v, 0)
                    if v == HALF_W - 1:
                        turn_back(w, v, 1)

            def product(n, lhs_hi, lhs_lo, before, open_=True, close=True, sums_before=None):
                for k in range(KT):
                    pe.wait_ge(w_lo_done, 8 * n + k + 1)
                    if sums_before is not None:
                        pe.wait_ge(g_drained, sums_before + 1 + 2 * (k + 1))
                    for t in range(NT):
                        if k == 0 and open_ and before is not None:
                            pe.wait_ge(u_drained, before + t + 1)
                        product_item(k, t, lhs_hi, lhs_lo, open_ and k == 0, close and k == KT - 1)

            pe.wait_ge(turned_read, 2 * WINDOWS + 1)
            pe.wait_ge(diag_done, 1)
            for c in range(2):
                last = mm(bank(5 + c, c=SPLIT), ones[:, :], diag[:, :, :].rearrange("p a b -> p (a b)")[:, c * SPLIT:(c + 1) * SPLIT],
                          start=True, stop=True)
            last.then_inc(ar_bcast, 1)
            pe.wait_ge(att_done, NT)
            for d in range(NT):
                if d >= 3:
                    pe.wait_ge(attT_lo_done, d - 2)
                for t in range(NT):
                    last = nc.tensor.transpose(pair(d % 3)[:, t * P:t * P + rows(t)], att[0:rows(t), t, d * P:(d + 1) * P],
                                               ident[0:rows(t), 0:rows(t)])
                last.then_inc(attT_ready, 1)
            pe.wait_ge(attT_lo_done, NT)
            for t in range(NT):
                if t >= 3:
                    pe.wait_ge(hp_read, t - 2)
                c = slice(t * P, t * P + rows(t))
                for half in range(2):
                    o = bank(2 * (t % 3) + half, rows(t))
                    for d in range(NT):
                        k = slice(0, rows(d))
                        mm(o, M_hi[0][k, d, c], h_parts[k, 2 * half, d, :], start=d == 0, stop=False)
                        mm(o, M_lo[0][k, d, c], h_parts[k, 2 * half, d, :], start=False, stop=False)
                        last = mm(o, M_hi[0][k, d, c], h_parts[k, 2 * half + 1, d, :], start=False, stop=d == NT - 1)
                last.then_inc(hp_ready, 1)
            for t in range(NT):
                pe.wait_ge(x1_done, t + 1)
                if t >= 3:
                    pe.wait_ge(x1T_lo_done, t - 2)
                for k in range(KT):
                    last = nc.tensor.transpose(pair(t % 3)[:, k * P:k * P + rows(t)], u[0:rows(t), t, k * P:(k + 1) * P],
                                               ident[0:rows(t), 0:rows(t)])
                last.then_inc(x1T_ready, 1)
            pe.wait_ge(x1T_lo_done, NT)

            def aggregate(i, half):
                if half == 0:
                    pe.wait_ge(C_ready, i + 1)
                    pe.wait_ge(g_drained, ITEMS * (i + 1))
                    for t in range(NT):
                        for m in range(NT):
                            last = mm(bank(5, c0=2 * t, c=2), C_hi[:, m, t * P:(t + 1) * P], ones_r[:, 0:2],
                                      start=m == 0, stop=m == NT - 1)
                    last.then_inc(g_ready, 1)
                for e in range(half * SUMS // 2, (half + 1) * SUMS // 2):
                    c0, cn = NCOL[e % 2]
                    f = slice(e // 2 * P, e // 2 * P + P)
                    o = bank(5 + (e + 1) % GB, c=cn)
                    if e + 1 >= GB:
                        pe.wait_ge(g_drained, ITEMS * (i + 1) + e + 2 - GB)
                    for m in range(NT):
                        r = slice(0, rows(m))
                        mm(o, x1_hi[r, m, f], C_hi[r, m, c0:c0 + cn], start=m == 0, stop=False)
                        last = mm(o, x1_lo[r, m, f], C_hi[r, m, c0:c0 + cn], start=False, stop=m == NT - 1)
                    last.then_inc(g_ready, 1)

            def step_work(i, odd):
                for half in range(2):
                    n = 2 * i + SEG_U + half
                    product(n, M_hi[odd], M_lo[odd], 2 * NT * i + NT * (SEG_U + half),
                            sums_before=ITEMS * i if half == 0 else None)
                    aggregate(i, half)

            with pe.Fori(0, R // 2) as j:
                for s in range(2):
                    step_work(2 * j + s, s)
            for half in range(2):
                n = SEG_U + 2 * R + half
                product(n, M_hi[0], M_lo[0], NT * n, sums_before=ITEMS * R if half == 0 else None)
                for t, kh in [(t, kh) for t in range(NT) for kh in range(2)][half * NT:(half + 1) * NT]:
                    for lo_, src in enumerate((x1_hi, x1_lo)):
                        it = 2 * (2 * t + kh) + lo_
                        if it >= GB:
                            b4 = it - GB
                            pe.wait_ge(xt2_lo_done if b4 % 2 else xt2_hi_done, b4 // 2 + 1)
                        elif it == 0:
                            pe.wait_ge(g_drained, ITEMS * (R + 1))
                        for k in range(4):
                            f = slice((4 * kh + k) * P, (4 * kh + k + 1) * P)
                            last = nc.tensor.transpose(bank(5 + it % GB, c0=k * P, c=rows(t)),
                                                       src[0:rows(t), t, f].bitcast(f32), ident[0:rows(t), 0:rows(t)])
                        last.then_inc(xt2_ready, 1)
            pe.wait_ge(xt2_lo_done, 2 * NT)
            pe.wait_ge(xt2_hi_done, 2 * NT)
            product(SEG_G, M_hi[1], M_lo[1], BANKS_G, close=False)
            for t in range(NT):
                for kh in range(2):
                    it = 2 * t + kh
                    if it >= GB:
                        pe.wait_ge(uT_lo_done, it - GB + 1)
                    for k in range(4):
                        last = nc.tensor.transpose(bank(5 + it % GB, c0=k * P, c=rows(t)),
                                                   u[0:rows(t), t, (4 * kh + k) * P:(4 * kh + k + 1) * P],
                                                   ident[0:rows(t), 0:rows(t)])
                    last.then_inc(uT_ready, 1)
            pe.wait_ge(uT_lo_done, 2 * NT)
            product(SEG_G + 1, M_hi[0], M_lo[0], None, open_=False)
            product(SEG_G + 2, M_hi[1], M_lo[1], BANKS_G + NT, close=False)
            product(SEG_G + 3, M_hi[0], M_lo[0], None, open_=False)


def kernel(**inputs):
    import numpy as np
    import concourse.bacc as bacc
    from concourse import mybir
    from concourse.bass_utils import run_bass_kernel_spmd

    x = np.ascontiguousarray(inputs["x"])
    n, d = x.shape
    relations = inputs["L1_gnn_weight"].shape[0]
    edges = inputs["dst"].shape[0]
    tiles = 2 * -(-edges // 256)
    far = 1 << 20

    def padded(v, fill):
        row = np.full((tiles * 128,), fill, np.int32)
        row[:edges] = v
        return row

    dst = padded(inputs["dst"], far)
    w_gate = np.asarray(inputs["L1_gnn_w_gate"])
    arrays = {
        "dst_cols": np.ascontiguousarray(dst.reshape(tiles, 128).T),
        "src_cols": np.ascontiguousarray(padded(inputs["src"], 0).reshape(tiles, 128).T),
        "type_cols": np.ascontiguousarray(padded(inputs["edge_type_8"], 0).reshape(tiles, 128).T),
        "dst_units": dst.reshape(tiles // 2, 256),
        "xT": np.ascontiguousarray(x.T),
        "x": x,
        "weights": np.concatenate([np.asarray(inputs["L0_gnn_W"]), np.asarray(inputs["L1_gnn_root"]),
                                   np.asarray(inputs["L1_gnn_weight"]).reshape(relations * d, d), w_gate]),
        "a": np.ascontiguousarray(inputs["L0_gnn_a"]),
        "bias": np.ascontiguousarray(inputs["L1_gnn_bias"]),
        "b_gate": np.ascontiguousarray(inputs["L1_gnn_b_gate"]),
    }
    nc = bacc.Bacc("TRN2", target_bir_lowering=False, num_devices=1)
    args = [nc.dram_tensor(name, v.shape, mybir.dt.from_np(v.dtype), kind="ExternalInput").ap() for name, v in arrays.items()]
    counts = nc.dram_tensor("counts_dram", (relations, -(-n // 128), 128, 128 * -(-n // 128)), mybir.dt.int16, kind="Internal").ap()
    out = nc.dram_tensor("out", (n, d), mybir.dt.float32, kind="ExternalOutput").ap()
    gat_rgcn_kernel(nc, *args, counts, out)
    return run_bass_kernel_spmd(nc, [arrays], core_ids=[0]).results[0]["out"]
```
